# Optimizing a Trainium2 kernel written in Bass

```python
import numpy as np
import jax
import jax.numpy as jnp

def _softmax(x, axis=-1):
    return jax.nn.softmax(x, axis=axis)

def _gelu(x):
    return jax.nn.gelu(x, approximate=True)

def _silu(x):
    return jax.nn.silu(x)

def _sigmoid(x):
    return jax.nn.sigmoid(x)

def _layernorm(x, axis=-1, eps=1e-05):
    m = jnp.mean(x, axis=axis, keepdims=True)
    v = jnp.var(x, axis=axis, keepdims=True)
    return (x - m) / jnp.sqrt(v + eps)

def _scatter_add(tgt, idx, src, axis=0):
    return tgt.at[idx].add(src)

def _segment_sum(src, seg, n):
    return jax.ops.segment_sum(src, seg, n)
kernel_name = 'mk_gps_d1_gnn_r8_56791c'

def setup_inputs(seed: int=0):
    np.random.seed(seed)
    _w = jnp.asarray

    def _rec_inputs():
        import jax
        import jax.numpy as jnp
        _gk = jax.random.key(seed)
        x = -0.0002117 + 1 * jax.random.normal(jax.random.fold_in(_gk, 1), (1250, 512), jnp.float32)
        _s = jax.random.randint(jax.random.fold_in(_gk, 2), (10000,), 0, 1250, jnp.int32)
        _d = jax.random.randint(jax.random.fold_in(_gk, 3), (10000,), 0, 1250, jnp.int32)
        _loop = jnp.arange(1250, dtype=jnp.int32)
        src = jnp.concatenate([_s, _d, _loop])
        dst = jnp.concatenate([_d, _s, _loop])
        _o = jnp.argsort(dst, stable=True)
        src = src[_o]
        dst = dst[_o]
        return (x, src, dst)
    x, src, dst = _rec_inputs()

    def _L0_gnn_setup():
        import jax, jax.numpy as jnp
        import numpy as np
        N = 6250
        IN_CH = 512
        OUT_CH = 512
        DEG = 32
        E = N * DEG
        key = jax.random.key(seed)
        kx, kwc, kwn, kb, ke = jax.random.split(key, 5)
        x = jax.random.normal(kx, (N, IN_CH), dtype=jnp.float32)
        bound = 1.0 / np.sqrt(IN_CH)
        wc = jax.random.uniform(kwc, (IN_CH, OUT_CH), minval=-bound, maxval=bound, dtype=jnp.float32)
        wn = jax.random.uniform(kwn, (IN_CH, OUT_CH), minval=-bound, maxval=bound, dtype=jnp.float32)
        bias = jax.random.uniform(kb, (OUT_CH,), minval=-bound, maxval=bound, dtype=jnp.float32)
        src = jnp.repeat(jnp.arange(N, dtype=jnp.int64), DEG)
        dst = jax.random.randint(ke, (E,), 0, N, dtype=jnp.int64)
        edge_index = jnp.stack([src, dst], axis=0)
        return {'x': x, 'wc': wc, 'wn': wn, 'bias': bias, 'edge_index': edge_index}
    _L0_gnn_all = _L0_gnn_setup()
    _L0_gnn_in = {k: v for k, v in _L0_gnn_all.items() if k in ('wc', 'wn', 'bias')}
    del _L0_gnn_all

    def _L0_mix_setup():
        import jax, jax.numpy as jnp
        import numpy as np
        HEADS = 8
        DIM_HEAD = 64
        EPS = 1e-05

        def layer_norm(x, gamma):
            mu = jnp.mean(x, axis=-1, keepdims=True)
            var = jnp.var(x, axis=-1, keepdims=True)
            return (x - mu) * jax.lax.rsqrt(var + EPS) * gamma
        key = jax.random.key(seed)
        k1, k2, k3 = jax.random.split(key, 3)
        b, n, dim = (4, 2048, 512)
        hidden = HEADS * DIM_HEAD
        x = jax.random.normal(k1, (b, n, dim), dtype=jnp.float32)
        norm_gamma = jnp.ones((dim,), dtype=jnp.float32)
        w_qkv = jax.random.normal(k2, (hidden * 3, dim), dtype=jnp.float32) * dim ** (-0.5)
        w_out = jax.random.normal(k3, (dim, hidden), dtype=jnp.float32) * hidden ** (-0.5)
        out_gamma = jnp.ones((dim,), dtype=jnp.float32)
        return {'x': x, 'norm_gamma': norm_gamma, 'w_qkv': w_qkv, 'w_out': w_out, 'out_gamma': out_gamma}
    _L0_mix_all = _L0_mix_setup()
    _L0_mix_in = {k: v for k, v in _L0_mix_all.items() if k in ('norm_gamma', 'w_qkv', 'w_out', 'out_gamma')}
    del _L0_mix_all

    def _L0_ffn_setup():
        import jax, jax.numpy as jnp
        import numpy as np
        DIM = 512
        FFN_DIM = 1408
        GROUP = 128
        EPS = 1e-05

        def _quantize_weight(w, group_size):
            o, i = w.shape
            wg = w.reshape(o, i // group_size, group_size)
            scale = jnp.mean(jnp.abs(wg), axis=-1, keepdims=True) + EPS
            wq = jnp.clip(jnp.round(wg / scale), -1.0, 1.0) * scale
            return wq.reshape(o, i)

        def _bitlinear(x, w, group_size=GROUP):
            wq = w + jax.lax.stop_gradient(_quantize_weight(w, group_size) - w)
            return jnp.einsum('bsd,fd->bsf', x, wq)
        key = jax.random.key(seed)
        k_x, k_g, k_u, k_d = jax.random.split(key, 4)
        x = jax.random.normal(k_x, (8, 512, DIM), dtype=jnp.float32)
        sd_in = 1.0 / np.sqrt(DIM)
        sd_ffn = 1.0 / np.sqrt(FFN_DIM)
        w_gate = jax.random.normal(k_g, (FFN_DIM, DIM), dtype=jnp.float32) * sd_in
        w_up = jax.random.normal(k_u, (FFN_DIM, DIM), dtype=jnp.float32) * sd_in
        w_down = jax.random.normal(k_d, (DIM, FFN_DIM), dtype=jnp.float32) * sd_ffn
        return {'x': x, 'w_gate': w_gate, 'w_up': w_up, 'w_down': w_down}
    _L0_ffn_all = _L0_ffn_setup()
    _L0_ffn_in = {k: v for k, v in _L0_ffn_all.items() if k in ('w_gate', 'w_up', 'w_down')}
    del _L0_ffn_all
    return {'x': x, 'src': src, 'dst': dst, 'L0_gnn_wc': _L0_gnn_in['wc'], 'L0_gnn_wn': _L0_gnn_in['wn'], 'L0_gnn_bias': _L0_gnn_in['bias'], 'L0_mix_norm_gamma': _L0_mix_in['norm_gamma'], 'L0_mix_w_qkv': _L0_mix_in['w_qkv'], 'L0_mix_w_out': _L0_mix_in['w_out'], 'L0_mix_out_gamma': _L0_mix_in['out_gamma'], 'L0_ffn_w_gate': _L0_ffn_in['w_gate'], 'L0_ffn_w_up': _L0_ffn_in['w_up'], 'L0_ffn_w_down': _L0_ffn_in['w_down']}

def reference(x, src, dst, L0_gnn_wc, L0_gnn_wn, L0_gnn_bias, L0_mix_norm_gamma, L0_mix_w_qkv, L0_mix_w_out, L0_mix_out_gamma, L0_ffn_w_gate, L0_ffn_w_up, L0_ffn_w_down):
    import jax
    import jax.numpy as jnp

    def _L0_gnn_ref(x, wc, wn, bias, edge_index):
        import jax, jax.numpy as jnp
        import numpy as np
        N = 6250
        IN_CH = 512
        OUT_CH = 512
        DEG = 32
        E = N * DEG
        alpha = x @ wc
        beta = x @ wn
        src, dst = (edge_index[0], edge_index[1])
        sums = jax.ops.segment_sum(beta[dst], src, num_segments=x.shape[0])
        counts = jax.ops.segment_sum(jnp.ones_like(src, dtype=beta.dtype), src, num_segments=x.shape[0])
        gamma = sums / counts[:, None]
        return alpha + gamma + bias

    def _L0_mix_ref(x, norm_gamma, w_qkv, w_out, out_gamma):
        import jax, jax.numpy as jnp
        import numpy as np
        HEADS = 8
        DIM_HEAD = 64
        EPS = 1e-05

        def layer_norm(x, gamma):
            mu = jnp.mean(x, axis=-1, keepdims=True)
            var = jnp.var(x, axis=-1, keepdims=True)
            return (x - mu) * jax.lax.rsqrt(var + EPS) * gamma
        b, n, dim = x.shape
        h, d = (HEADS, DIM_HEAD)
        scale = d ** (-0.5)
        x = layer_norm(x, norm_gamma)
        qkv = jnp.einsum('bnc,fc->bnf', x, w_qkv)
        q, k, v = jnp.split(qkv, 3, axis=-1)
        to_bhnd = lambda t: t.reshape(b, n, h, d).transpose(0, 2, 1, 3)
        q, k, v = (to_bhnd(q), to_bhnd(k), to_bhnd(v))
        q = jax.nn.softmax(q, axis=-1) * scale
        k = jax.nn.softmax(k, axis=-2)
        context = jnp.einsum('bhnd,bhne->bhde', k, v)
        out = jnp.einsum('bhde,bhnd->bhne', context, q)
        out = out.transpose(0, 2, 1, 3).reshape(b, n, h * d)
        out = jnp.einsum('bnf,cf->bnc', out, w_out)
        return layer_norm(out, out_gamma)

    def _L0_ffn_ref(x, w_gate, w_up, w_down):
        import jax, jax.numpy as jnp
        import numpy as np
        DIM = 512
        FFN_DIM = 1408
        GROUP = 128
        EPS = 1e-05

        def _quantize_weight(w, group_size):
            o, i = w.shape
            wg = w.reshape(o, i // group_size, group_size)
            scale = jnp.mean(jnp.abs(wg), axis=-1, keepdims=True) + EPS
            wq = jnp.clip(jnp.round(wg / scale), -1.0, 1.0) * scale
            return wq.reshape(o, i)

        def _bitlinear(x, w, group_size=GROUP):
            wq = w + jax.lax.stop_gradient(_quantize_weight(w, group_size) - w)
            return jnp.einsum('bsd,fd->bsf', x, wq)
        gate = _bitlinear(x, w_gate)
        up = _bitlinear(x, w_up)
        h = jax.nn.silu(gate) * up
        return _bitlinear(h, w_down)
    edge_index = jnp.stack([src, dst])
    xn = _layernorm(x, axis=-1)
    x = x + _L0_gnn_ref(xn, L0_gnn_wc, L0_gnn_wn, L0_gnn_bias, edge_index) + _L0_mix_ref(xn[None], L0_mix_norm_gamma, L0_mix_w_qkv, L0_mix_w_out, L0_mix_out_gamma)[0]
    x = x + _L0_ffn_ref(_layernorm(x, axis=-1)[None], L0_ffn_w_gate, L0_ffn_w_up, L0_ffn_w_down)[0]
    return x

_drawn_inputs = setup_inputs


def setup_inputs(seed=0):
    import zlib

    import numpy as np

    out = dict(_drawn_inputs(seed))
    spreads = {'L0_mix_norm_gamma': (1.0, 0.2), 'L0_mix_out_gamma': (1.0, 0.2)}
    factors = {'L0_gnn_bias': 3.627}
    for name, (base, spread) in spreads.items():
        noise = np.random.default_rng([zlib.crc32(name.encode()), seed]).standard_normal(out[name].shape)
        drawn = base * np.exp(spread * noise) if base else spread * noise
        out[name] = jnp.asarray(drawn.astype(out[name].dtype))
    for name, factor in factors.items():
        out[name] = (out[name] * factor).astype(out[name].dtype)
    return out
```

```python
from contextlib import ExitStack

import concourse.bass as bass
from concourse import mybir

F32 = mybir.dt.float32
F16 = mybir.dt.float16
I32 = mybir.dt.int32
ALU = mybir.AluOpType
ACT = mybir.ActivationFunctionType
AX = mybir.AxisListType

EPS = 1e-5
W_SCALE = 64.0
X_SCALE = 32.0
Q_SCALE = 64.0
C_SCALE = 256.0
H_SCALE = 16.0
HEAD = 64
PARTS = ((0, 0), (1, 0), (0, 1))


def gps_layer(nc, x, src, dst, wc, wn, bias, g_norm, w_qkv, w_out, g_out, w_gate, w_up, w_down, out):
    N, D = x.shape
    E, = src.shape
    F = w_gate.shape[0]
    P = 125
    NT = N // P
    K = D // 128
    FT = F // 128
    HEADS = D // HEAD
    GRP = 4
    NG = -(-E // (GRP * P))
    LAST = E - (NG - 1) * GRP * P
    NC3 = [(0, 417), (417, 417), (834, 416)]
    MIX = 1.0 / (Q_SCALE * C_SCALE * HEAD ** 0.5)
    assert N == NT * P and D == 512 and w_qkv.shape[0] == 3 * D and F == FT * 128

    with ExitStack() as ctx:
        def sb(name, shape, dt):
            return ctx.enter_context(nc.sbuf_tensor(name, shape, dt))

        def sem(name):
            return ctx.enter_context(nc.semaphore(name))

        bank = [ctx.enter_context(nc.psum_tensor(f"bank{i}", [128, 512], F32)) for i in range(8)]

        ident = sb("ident", [128, 128], F32)
        iota_n = sb("iota_n", [P, N], F16)
        iota_b = sb("iota_b", [P, P], F16)
        block_at = sb("block_at", [NG, NT], F32)
        group_no = sb("group_no", [NG, 1], F32)
        ones_h = sb("ones_h", [P, 1], F16)
        halfpow = sb("halfpow", [P, NT], F32)
        bias_b = sb("bias_b", [P, D], F32)
        gout_b = bias_b
        grow = sb("grow", [K, 128], F32)
        gcol = sb("gcol", [128, K], F32)
        st6 = sb("st6", [P, NT, 6], F32)
        mv = sb("mv", [P, NT, 2], F32)
        rstd = sb("rstd", [P, NT], F32)
        nvar = sb("nvar", [P, NT], F32)
        r2k = sb("r2k", [P, NT], F32)
        r2v = sb("r2v", [P, NT], F32)
        qmx = sb("qmx", [P, HEADS], F32)
        qsum = sb("qsum", [P, HEADS], F32)
        kmaxc = sb("kmaxc", [128, K], F32)
        krec = sb("krec", [128, K], F32)
        stat = sb("stat", [P, 16], F32)
        xr = sb("xr", [P, NT, D], F32)
        betas = sb("betas", [P, 2, NT, D], F16)
        qT = sb("qT", [128, 2, K, NT * P], F16)
        w2 = sb("w2", [128, 2, K, D], F16)
        xn = sb("xn", [P, 2, D], F32)
        zone = sb("zone", [128, 27730], F32)
        small = sb("small", [128, 2560], F32)

        def view(at, shape, dt, zone=zone):
            n = 1
            for s in shape[1:]:
                n *= s
            words = n if dt != F16 else n // 2
            v = zone[0:shape[0], at:at + words]
            if dt != F32:
                v = v.bitcast(dt)
            names = "abcd"[:len(shape) - 1]
            if len(shape) > 2:
                v = v.rearrange(f"p ({' '.join(names)}) -> p {' '.join(names)}", **{c: s for c, s in zip(names, shape[1:])})
            return v
        kf = view(0, [P, NT, D], F32)
        vp = view(5120, [P, 2, NT, K, 130], F16)
        ek = view(10320, [P, 2, NT, D], F16)
        wcn = view(15440, [128, 2, K, 2 * D], F16)
        wqkvT = view(19536, [128, 2, K, 3 * D], F16)
        raw = view(25680, [128, K, D], F32)
        qe = view(0, [P, D], F32, small)
        qn = view(512, [P, D], F32, small)
        xT = view(1024, [128, 2, 2, K, P], F16, small)
        kmax = view(2040, [P, D], F32, small)
        wzone = sb("wzone", [128, 2048], F32)
        woutT = view(0, [128, 2, K, D], F16, wzone)
        ctxn = sb("ctxn", [128, 128], F32)
        ctxT = sb("ctxT", [128, 2, 128], F16)
        counts = view(0, [P, 2, NT, N], F16)
        oh_src = view(12500, [P, GRP, N], F16)
        oh_dst = view(15000, [P, GRP, 128], F16)
        eT = view(15256, [P, NG, GRP * 2], F32)
        edges_i = view(15600, [NG, 2, GRP * P], I32)
        edges = view(16600, [NG, 2, GRP * P], F32)
        ov = view(17600, [NG, 4, NT], F32)
        hT = view(0, [128, 2, FT, N], F16)
        wdT = view(13750, [128, 2, FT, D], F16)
        wraw = view(19382, [128, 2, 12, 128], F32)
        wa = view(22454, [128, 2, 12, 128], F32)
        wb = view(25526, [128, 12, 128], F32)
        wgu = view(0, [128, 2, 2, 2 * K * 128], F16, wzone)
        gsum = sb("gsum", [128, 2, 12], F32)
        gthr = sb("gthr", [128, 3, 12], F32)
        sg = view(0, [128, 2, 417], F32, small)
        hf = view(834, [128, 2, 417], F32, small)

        ext = sb("ext", [NG, 4], F32)
        bounds = sb("bounds", [NT, 3], F32)
        brow = sb("brow", [1, 2 * NT], I32)

        names = """gT_mm gout_in v_own x_in w_in wqkv_in small_in g_const g_ident edge_in stats_v stats_p r_ready
            prep_T prep_hi prep_lo wcn_hi wcn_lo pvec
            xn_ready xT_done xT_hi xT_lo beta_mm k_mm v_mm q_mm alpha_mm
            beta_hi beta_lo k_out kmax_d v_hi v_lo q_max q_sub q_exp q_sum q_rec q_norm qT_mm qT_hi qT_lo
            xb_done acc_done kmT_mm kmc_d kmb_mm k_sub k_exp ek_hi ek_lo v_one ctx_mm ctx_rec ctx_n ctxT_mm
            ctx_hi ctx_lo ctx_zero w2_mm w2_hi w2_lo edge_f eT_done bound_v bT_mm bp_mm brow_d fill_d
            iota_d oh_ready oh_used cnt_mm cnt_hi cnt_lo gam_mm cn_mm mix_mm gam_d crec_d mst_v mst_p mst_w
            mix_n mix_g x1_d x1_st x1_p x2_n x2T_mm x2_hi x2_lo wr_in0 wr_in1 wr_abs wr_thr wr_a wr_b wr_q wr_T
            wr_hi wr_lo gu_mm sg_d hf_d h_hi h_lo dn_mm dn_d out_d""".split()
        S = {n: sem(n) for n in names}

        block = ctx.enter_context(nc.Block())

        @block.sync
        def _(sp):
            sp.dma_start(bias_b[:], bias.rearrange("(a d) -> a d", a=1).broadcast_to([P, D])).then_inc(S["small_in"], 16)
            sp.dma_start(grow[:], g_norm.rearrange("(k p) -> k p", p=128)).then_inc(S["small_in"], 16)
            for t in range(NT):
                sp.dma_start(xr[:, t, :], x[t * P:(t + 1) * P, :]).then_inc(S["x_in"], 16)
            for g in range(4):
                if g:
                    sp.wait_ge(S["prep_T"], 4 * g)
                w = w_qkv[g * D:(g + 1) * D, :] if g < 3 else w_out
                sp.dma_start(raw, w.rearrange("(j p) c -> p j c", p=128)).then_inc(S["wqkv_in"], 16)
            sp.wait_ge(S["prep_T"], 16)
            for g, w in enumerate((wc, wn)):
                if g:
                    sp.wait_ge(S["wcn_hi"], 1)
                    sp.wait_ge(S["wcn_lo"], 1)
                sp.dma_start(raw, w.rearrange("(k p) o -> p k o", p=128)).then_inc(S["w_in"], 16)
            sp.wait_ge(S["xb_done"], NT)
            sp.dma_start(gout_b[:], g_out.rearrange("(a d) -> a d", a=1).broadcast_to([P, D])).then_inc(S["gout_in"], 16)
            sp.wait_ge(S["fill_d"], 1)
            sp.dma_start(edges_i[0:NG - 1, 0, :], src[0:(NG - 1) * GRP * P].rearrange("(g e) -> g e", e=GRP * P)).then_inc(S["edge_in"], 16)
            sp.dma_start(edges_i[0:NG - 1, 1, :], dst[0:(NG - 1) * GRP * P].rearrange("(g e) -> g e", e=GRP * P)).then_inc(S["edge_in"], 16)
            sp.dma_start(edges_i[NG - 1:NG, 0, 0:LAST], src[E - LAST:E].rearrange("(g e) -> g e", g=1)).then_inc(S["edge_in"], 16)
            sp.dma_start(edges_i[NG - 1:NG, 1, 0:LAST], dst[E - LAST:E].rearrange("(g e) -> g e", g=1)).then_inc(S["edge_in"], 16)
            sp.wait_ge(S["x2_lo"], NT)
            for i in range(FT):
                if i >= 2:
                    sp.wait_ge(S["wr_a"], i - 1)
                    sp.wait_ge(S["wr_b"], i - 1)
                f = slice(i * 128, (i + 1) * 128)
                sp.dma_start(wraw[:, i % 2, 0:4, :], w_gate[f, :].rearrange("p (k d) -> p k d", d=128)).then_inc(S[f"wr_in{i % 2}"], 16)
                sp.dma_start(wraw[:, i % 2, 4:8, :], w_up[f, :].rearrange("p (k d) -> p k d", d=128)).then_inc(S[f"wr_in{i % 2}"], 16)
                sp.dma_start(wraw[:, i % 2, 8:12, :], w_down[:, f].rearrange("(k p) d -> p k d", p=128)).then_inc(S[f"wr_in{i % 2}"], 16)
            for t in range(NT):
                sp.wait_ge(S["dn_d"], t + 1)
                sp.dma_start(out[t * P:(t + 1) * P, :], xr[:, t, :]).then_inc(S["out_d"], 16)
            sp.wait_ge(S["out_d"], 16 * NT)

        @block.gpsimd
        def _(g):
            g.memset(ident[:], 0.0).then_inc(S["g_ident"], 1)
            g.wait_ge(S["g_ident"], 1)
            g.affine_select(out=ident[:], in_=ident[:], compare_op=ALU.not_equal, fill=1.0, base=0,
                            pattern=[[-1, 128]], channel_multiplier=1).then_inc(S["g_ident"], 1)
            g.iota(iota_n[:], [[1, N]], base=0, channel_multiplier=0, allow_small_or_imprecise_dtypes=True).then_inc(S["g_const"], 1)
            g.iota(block_at[:], [[P, NT]], base=0, channel_multiplier=0, allow_small_or_imprecise_dtypes=True).then_inc(S["g_const"], 1)
            g.iota(group_no[:], [[1, 1]], base=1, channel_multiplier=1, allow_small_or_imprecise_dtypes=True).then_inc(S["g_const"], 1)
            g.memset(ones_h[:], 1.0).then_inc(S["g_const"], 1)
            g.memset(halfpow[:], -0.5).then_inc(S["g_const"], 1)
            g.memset(ctxT[:], 0.0).then_inc(S["ctx_zero"], 1)
            g.wait_ge(S["g_const"], 5)
            n = [0]

            def step(ins):
                n[0] += 1
                ins.then_inc(S["pvec"], 1)
                g.wait_ge(S["pvec"], n[0])

            g.wait_ge(S["stats_v"], NT)
            step(g.tensor_scalar(nvar[:], mv[:, :, 1], EPS, None, ALU.add))
            step(g.tensor_tensor(rstd[:], nvar[:], halfpow[:], ALU.pow))
            step(g.tensor_tensor(nvar[:], rstd[:], rstd[:], ALU.mult))
            step(g.tensor_tensor(nvar[:], nvar[:], mv[:, :, 1], ALU.mult))
            step(g.tensor_scalar(nvar[:], nvar[:], EPS, None, ALU.add))
            step(g.tensor_tensor(r2k[:], nvar[:], halfpow[:], ALU.pow))
            step(g.tensor_scalar(r2v[:], r2k[:], X_SCALE / (W_SCALE * X_SCALE), None, ALU.mult))
            g.tensor_scalar(r2k[:], r2k[:], 1.0 / (W_SCALE * X_SCALE), None, ALU.mult).then_inc(S["r_ready"], 1)
            for h in range(2):
                g.memset(vp[:, h, :, :, 128:129].rearrange("p t k o -> p (t k) o"), 1.0 - h).then_inc(S["v_one"], 1)
            g.wait_ge(S["small_in"], 32)
            for t in range(NT):
                g.wait_ge(S["xn_ready"], t + 1)
                g.tensor_tensor(xr[:, t, :], xr[:, t, :], bias_b[:], ALU.add).then_inc(S["xb_done"], 1)
            for t in range(NT):
                g.wait_ge(S["ek_hi"], t + 1)
                g.tensor_tensor(ek[:, 1, t, :], kf[:, t, :], ek[:, 0, t, :], ALU.subtract).then_inc(S["ek_lo"], 1)
            def rsqrt(dst_ap, var_ap, scale2, m, sem_in, k_in, sem_out):
                g.wait_ge(sem_in, k_in)
                step(g.tensor_scalar(stat[:, m:m + 1], var_ap, scale2, EPS, ALU.mult, ALU.add))
                g.tensor_tensor(dst_ap, stat[:, m:m + 1], halfpow[:, 0:1], ALU.pow).then_inc(sem_out, 1)

            for t in range(NT):
                rsqrt(stat[:, 1:2], stat[:, 5:6], MIX * MIX, 0, S["mst_v"], t + 1, S["mst_p"])
                g.wait_ge(S["mix_n"], t + 1)
                if t == 0:
                    g.wait_ge(S["gout_in"], 16)
                g.tensor_tensor(xn[:, 0, :], xn[:, 0, :], gout_b[:], ALU.mult).then_inc(S["mix_g"], 1)
                rsqrt(stat[:, 9:10], stat[:, 13:14], 1.0, 8, S["x1_st"], t + 1, S["x1_p"])
            for i in range(FT):
                g.wait_ge(S["wr_thr"], i + 1)
                g.wait_ge(S[f"wr_in{i % 2}"], 48 * (i // 2 + 1))
                if i:
                    g.wait_ge(S["wr_q"], i)
                for j in range(12):
                    ins = g.tensor_scalar(wb[:, j, :], wraw[:, i % 2, j, :], gthr[:, 2, j:j + 1], gthr[:, 0, j:j + 1], ALU.is_lt, ALU.mult)
                ins.then_inc(S["wr_b"], 1)
                g.wait_ge(S["wr_b"], i + 1)
                g.wait_ge(S["wr_a"], i + 1)
                g.tensor_tensor(wa[:, i % 2, :, :], wa[:, i % 2, :, :], wb, ALU.subtract).then_inc(S["wr_q"], 1)

        @block.tensor
        def _(pe):
            pe.wait_ge(S["g_ident"], 2)
            pe.wait_ge(S["small_in"], 32)
            pe.transpose(bank[7][:, 0:K], grow[:], ident[0:K, 0:K]).then_inc(S["gT_mm"], 1)
            for g in range(4):
                pe.wait_ge(S["wqkv_in"], 16 * (g + 1))
                for k in range(K):
                    n = 4 * g + k
                    if n >= 4:
                        pe.wait_ge(S["prep_hi"], n - 3)
                        pe.wait_ge(S["prep_lo"], n - 3)
                    for j in range(4):
                        i = pe.transpose(bank[n % 4][:, j * 128:(j + 1) * 128], raw[:, j, k * 128:(k + 1) * 128], ident[:])
                    i.then_inc(S["prep_T"], 1)
            pe.wait_ge(S["prep_hi"], 16)
            pe.wait_ge(S["prep_lo"], 16)
            pe.wait_ge(S["wcn_hi"], 2)
            pe.wait_ge(S["wcn_lo"], 2)

            def turn_x(t):
                pe.wait_ge(S["xn_ready"], t + 1)
                if t:
                    pe.wait_ge(S["xT_hi"], t)
                    pe.wait_ge(S["xT_lo"], t)
                for k in range(K):
                    i = pe.transpose(bank[5][:, k * P:(k + 1) * P], xn[:, t % 2, k * 128:(k + 1) * 128], ident[0:P, 0:P])
                i.then_inc(S["xT_done"], 1)

            def product(b, t, w, c0, done):
                n = 0
                for k in range(K):
                    for a, m in PARTS:
                        i = pe.matmul(b[0:P, :], xT[:, t % 2, a, k, :], w[:, m, k, c0:c0 + D], start=n == 0, stop=n == 3 * K - 1)
                        n += 1
                i.then_inc(done, 1)

            def turn_q(t):
                pe.wait_ge(S["q_norm"], t + 1)
                if t:
                    pe.wait_ge(S["qT_hi"], t)
                    pe.wait_ge(S["qT_lo"], t)
                for k in range(K):
                    i = pe.transpose(bank[6][:, k * P:(k + 1) * P], qn[:, k * 128:(k + 1) * 128], ident[0:P, 0:P])
                i.then_inc(S["qT_mm"], 1)

            turn_x(0)
            for t in range(NT):
                pe.wait_ge(S["xT_hi"], t + 1)
                pe.wait_ge(S["xT_lo"], t + 1)
                if t:
                    pe.wait_ge(S["k_out"], t)
                product(bank[1], t, wqkvT, D, S["k_mm"])
                if t:
                    pe.wait_ge(S["q_sub"], t)
                product(bank[3], t, wqkvT, 0, S["q_mm"])
                if t:
                    turn_q(t - 1)
                    pe.wait_ge(S["v_lo"], t)
                product(bank[2], t, wqkvT, 2 * D, S["v_mm"])
                if t + 1 < NT:
                    turn_x(t + 1)
                if t:
                    pe.wait_ge(S["beta_lo"], t)
                product(bank[0], t, wcn, D, S["beta_mm"])
                if t:
                    pe.wait_ge(S["acc_done"], t)
                product(bank[4], t, wcn, 0, S["alpha_mm"])
            turn_q(NT - 1)
            pe.wait_ge(S["kmax_d"], NT)
            for k in range(K):
                i = pe.transpose(bank[7][:, k * P:(k + 1) * P], kmax[:, k * 128:(k + 1) * 128], ident[0:P, 0:P])
            i.then_inc(S["kmT_mm"], 1)
            pe.wait_ge(S["kmc_d"], 1)
            for k in range(K):
                i = pe.matmul(bank[7][0:P, k * 128:(k + 1) * 128], kmaxc[:, k:k + 1].broadcast_to([128, P]), ident[:], start=True, stop=True)
            i.then_inc(S["kmb_mm"], 1)
            pe.wait_ge(S["v_one"], 2)
            pe.wait_ge(S["v_lo"], NT)
            pe.wait_ge(S["q_sub"], NT)
            pe.wait_ge(S["beta_lo"], NT)
            for t in range(NT):
                pe.wait_ge(S["ek_lo"], t + 1)
                for k in range(K):
                    for n, (a, m) in enumerate(PARTS):
                        i = pe.matmul(bank[k][:, 0:129], ek[:, a, t, k * 128:(k + 1) * 128], vp[:, m, t, k, 0:129],
                                      start=t == 0 and n == 0, stop=t == NT - 1 and n == 2)
            i.then_inc(S["ctx_mm"], 1)
            for k in range(K):
                pe.wait_ge(S["ctx_n"], k + 1)
                if k:
                    pe.wait_ge(S["ctx_lo"], k)
                pe.transpose(bank[4][:, 0:128], ctxn[:], ident[:]).then_inc(S["ctxT_mm"], 1)
                pe.wait_ge(S["ctx_hi"], k + 1)
                pe.wait_ge(S["ctx_lo"], k + 1)
                if k:
                    pe.wait_ge(S["w2_lo"], k)
                for n, (a, m) in enumerate(PARTS):
                    i = pe.matmul(bank[5][:, :], ctxT[:, a, :], woutT[:, m, k, :], start=n == 0, stop=n == 2)
                i.then_inc(S["w2_mm"], 1)

            pe.wait_ge(S["bound_v"], 1)
            for a in range(2):
                pe.transpose(bank[6][0:NT, a * NG:(a + 1) * NG], ov[:, 2 + a, :], ident[0:NG, 0:NG])
            for q in range(GRP):
                for a in range(2):
                    i = pe.transpose(bank[7][0:P, (q * 2 + a) * NG:(q * 2 + a + 1) * NG], edges[:, a, q * P:(q + 1) * P], ident[0:NG, 0:NG])
            i.then_inc(S["bT_mm"], 1)
            pe.wait_ge(S["bound_v"], 2)
            for a in range(2):
                i = pe.transpose(bank[0][0:1, a * NT:(a + 1) * NT], bounds[:, a:a + 1], ident[0:NT, 0:NT])
            i.then_inc(S["bp_mm"], 1)
            pe.wait_ge(S["brow_d"], 1)
            pe.wait_ge(S["w2_lo"], K)
            pe.nop().then_inc(S["oh_used"], GRP)
            visit = pe.alloc_register("pe_visit")
            pe.reg_mov(visit, 0)
            for b in range(NT):
                if b >= 2:
                    pe.wait_ge(S["cnt_lo"], 3 * (b - 1))
                hi = pe.value_load(brow[0:1, b:b + 1], min_val=3, max_val=NG)
                lo = pe.value_load(brow[0:1, b + NT:b + NT + 1], min_val=0, max_val=NG - 3)

                def group(first, last):
                    w = pe.snap(visit, min_val=0, max_val=NT * NG * GRP)
                    for q in range(GRP):
                        pe.wait_ge(S["oh_ready"], w + (q + 1))
                        for c, (n0, nn) in enumerate(NC3):
                            i = pe.matmul(bank[3 * (b % 2) + c][0:P, 0:nn], oh_dst[:, q, 0:P], oh_src[:, q, n0:n0 + nn],
                                          start=first and q == 0, stop=True, skip_group_check=True)
                        i.then_inc(S["oh_used"], 1)
                        if last and q == GRP - 1:
                            pe.matmul(bank[6][0:1, 0:1], ones_h[:], ones_h[:], start=True, stop=True).then_inc(S["cnt_mm"], 1)
                    pe.reg_add(visit, visit, GRP)

                group(True, False)
                with pe.Fori(lo + 1, hi - 1):
                    group(False, False)
                group(False, True)

            pe.wait_ge(S["qT_lo"], NT)
            pe.wait_ge(S["cnt_lo"], 3 * NT)

            def turn_x1(t):
                pe.wait_ge(S["x2_n"], t + 1)
                if t:
                    pe.wait_ge(S["x2_hi"], t)
                    pe.wait_ge(S["x2_lo"], t)
                for k in range(K):
                    i = pe.transpose(bank[6][:, k * P:(k + 1) * P], xn[:, 1, k * 128:(k + 1) * 128], ident[0:P, 0:P])
                i.then_inc(S["x2T_mm"], 1)

            for t in range(NT):
                if t >= 2:
                    pe.wait_ge(S["mix_n"], t - 1)
                n = 0
                for k in range(K):
                    for a, m in PARTS:
                        i = pe.matmul(bank[2 + t % 2][0:P, :], qT[:, a, k, t * P:(t + 1) * P], w2[:, m, k, :], start=n == 0, stop=n == 3 * K - 1)
                        n += 1
                i.then_inc(S["mix_mm"], 1)
                if t >= 2:
                    pe.wait_ge(S["gam_d"], t - 1)
                n = 0
                for m in range(NT):
                    for a, c in PARTS:
                        i = pe.matmul(bank[t % 2][0:P, :], counts[:, a, m, t * P:(t + 1) * P], betas[:, c, m, :], start=n == 0, stop=n == 3 * NT - 1)
                        n += 1
                i.then_inc(S["gam_mm"], 1)
                if t >= 2:
                    pe.wait_ge(S["crec_d"], t - 1)
                for m in range(NT):
                    for a in range(2):
                        i = pe.matmul(bank[4 + t % 2][0:P, 0:1], counts[:, a, m, t * P:(t + 1) * P], ones_h[:], start=m == 0 and a == 0, stop=m == NT - 1 and a == 1)
                i.then_inc(S["cn_mm"], 1)
                if t:
                    turn_x1(t - 1)
            turn_x1(NT - 1)

            pe.wait_ge(S["x2_hi"], NT)
            pe.wait_ge(S["x2_lo"], NT)
            pe.wait_ge(S["gam_d"], NT)

            def turn_w(i, g):
                pe.wait_ge(S["wr_q"], i + 1)
                n = 3 * i + g
                if n >= 2:
                    pe.wait_ge(S["wr_hi"], n - 1)
                    pe.wait_ge(S["wr_lo"], n - 1)
                for k in range(K):
                    ins = pe.transpose(bank[6 + n % 2][:, k * 128:(k + 1) * 128], wa[:, i % 2, 4 * g + k, :], ident[:])
                ins.then_inc(S["wr_T"], 1)

            for g in range(3):
                turn_w(0, g)
            u = 0
            for i in range(FT):
                pe.wait_ge(S["wr_hi"], 3 * i + 2)
                pe.wait_ge(S["wr_lo"], 3 * i + 2)
                for c, (n0, nn) in enumerate(NC3):
                    if u >= 3:
                        pe.wait_ge(S["hf_d"], u - 2)
                    for z in range(2):
                        n = 0
                        for k in range(K):
                            for a, m in PARTS:
                                ins = pe.matmul(bank[2 * c + z][:, 0:nn], wgu[:, i % 2, a, (z * K + k) * 128:(z * K + k + 1) * 128],
                                                qT[:, m, k, n0:n0 + nn], start=n == 0, stop=n == 3 * K - 1)
                                n += 1
                    ins.then_inc(S["gu_mm"], 1)
                    u += 1
                    if i + 1 < FT:
                        turn_w(i + 1, c)
            pe.wait_ge(S["h_hi"], 3 * FT)
            pe.wait_ge(S["h_lo"], 3 * FT)
            pe.wait_ge(S["wr_hi"], 3 * FT)
            pe.wait_ge(S["wr_lo"], 3 * FT)
            for t in range(NT):
                if t >= 2:
                    pe.wait_ge(S["dn_d"], t - 1)
                n = 0
                for i in range(FT):
                    for a, m in PARTS:
                        ins = pe.matmul(bank[t % 2][0:P, :], hT[:, a, i, t * P:(t + 1) * P], wdT[:, m, i, :], start=n == 0, stop=n == 3 * FT - 1)
                        n += 1
                ins.then_inc(S["dn_mm"], 1)

        @block.scalar
        def _(s):
            s.wait_ge(S["small_in"], 32)
            s.wait_ge(S["stats_v"], NT + 1)
            for g in range(4):
                for k in range(K):
                    n = 4 * g + k
                    s.wait_ge(S["prep_T"], n + 1)
                    if g < 3:
                        s.activation(wqkvT[:, 0, k, g * D:(g + 1) * D], bank[n % 4][:, :], ACT.Copy, scale=gcol[:, k:k + 1]).then_inc(S["prep_hi"], 1)
                    else:
                        s.activation(woutT[:, 0, k, :], bank[n % 4][:, :], ACT.Copy, scale=W_SCALE).then_inc(S["prep_hi"], 1)
            for g in range(2):
                s.wait_ge(S["w_in"], 16 * (g + 1))
                s.activation(wcn[:, 0, :, g * D:(g + 1) * D], raw, ACT.Copy, scale=W_SCALE).then_inc(S["wcn_hi"], 1)

            def xT_evac(t):
                s.wait_ge(S["xT_done"], t + 1)
                if t >= 2:
                    s.wait_ge(S["alpha_mm"], t - 1)
                s.activation(xT[:, t % 2, 0, :, :], bank[5][:, 0:K * P].rearrange("p (k n) -> p k n", k=K), ACT.Copy, scale=X_SCALE).then_inc(S["xT_hi"], 1)

            s.wait_ge(S["r_ready"], 1)
            xT_evac(0)
            for t in range(NT):
                s.wait_ge(S["k_mm"], t + 1)
                s.activation(kf[:, t, :], bank[1][0:P, :], ACT.Copy, scale=r2k[:, t:t + 1]).then_inc(S["k_out"], 1)
                s.wait_ge(S["q_sub"], t + 1)
                s.activation(qe[:], qe[:], ACT.Exp, scale=r2k[:, t:t + 1]).then_inc(S["q_exp"], 1)
                s.wait_ge(S["v_mm"], t + 1)
                s.activation(vp[:, 0, t, :, 0:128], bank[2][0:P, :].rearrange("p (k e) -> p k e", k=K), ACT.Copy, scale=r2v[:, t:t + 1]).then_inc(S["v_hi"], 1)
                if t + 1 < NT:
                    xT_evac(t + 1)
                s.wait_ge(S["beta_mm"], t + 1)
                s.activation(betas[:, 0, t, :], bank[0][0:P, :], ACT.Copy, scale=1.0 / W_SCALE).then_inc(S["beta_hi"], 1)
                s.wait_ge(S["qT_mm"], t + 1)
                s.activation(qT[:, 0, :, t * P:(t + 1) * P], bank[6][:, 0:K * P].rearrange("p (k n) -> p k n", k=K), ACT.Copy, scale=Q_SCALE).then_inc(S["qT_hi"], 1)
            for t in range(NT):
                s.wait_ge(S["k_sub"], t + 1)
                s.activation(kf[:, t, :], kf[:, t, :], ACT.Exp).then_inc(S["k_exp"], 1)
                s.wait_ge(S["k_exp"], t + 1)
                s.activation(ek[:, 0, t, :], kf[:, t, :], ACT.Copy).then_inc(S["ek_hi"], 1)
            s.wait_ge(S["ctx_zero"], 1)
            for k in range(K):
                s.wait_ge(S["ctxT_mm"], k + 1)
                if k:
                    s.wait_ge(S["w2_mm"], k)
                for h in range(2):
                    d = slice(64 * h, 64 * h + 64)
                    i = s.activation(ctxT[d, 0, d], bank[4][d, d], ACT.Copy, scale=C_SCALE)
                i.then_inc(S["ctx_hi"], 1)
                s.wait_ge(S["w2_mm"], k + 1)
                s.activation(w2[:, 0, k, :], bank[5][:, :], ACT.Copy, scale=1.0 / W_SCALE).then_inc(S["w2_hi"], 1)
            for b in range(NT):
                s.wait_ge(S["cnt_mm"], b + 1)
                for c, (n0, nn) in enumerate(NC3):
                    s.activation(counts[:, 0, b, n0:n0 + nn], bank[3 * (b % 2) + c][0:P, 0:nn], ACT.Copy).then_inc(S["cnt_hi"], 1)
            for t in range(NT):
                s.wait_ge(S["mst_w"], t + 1)
                if t:
                    s.wait_ge(S["x1_d"], t)
                s.activation(xn[:, 0, :], bank[2 + t % 2][0:P, :], ACT.Identity, bias=stat[:, 3:4], scale=stat[:, 2:3]).then_inc(S["mix_n"], 1)
                s.wait_ge(S["x2T_mm"], t + 1)
                s.activation(qT[:, 0, :, t * P:(t + 1) * P], bank[6][:, 0:K * P].rearrange("p (k n) -> p k n", k=K), ACT.Copy, scale=X_SCALE).then_inc(S["x2_hi"], 1)

            def w_evac(i, g):
                s.wait_ge(S["wr_T"], 3 * i + g + 1)
                if g < 2:
                    if i >= 2:
                        s.wait_ge(S["gu_mm"], 3 * (i - 1))
                    s.activation(wgu[:, i % 2, 0, g * D:(g + 1) * D], bank[6 + (3 * i + g) % 2][:, :], ACT.Copy, scale=W_SCALE).then_inc(S["wr_hi"], 1)
                else:
                    s.activation(wdT[:, 0, i, :], bank[6 + (3 * i + g) % 2][:, :], ACT.Copy, scale=W_SCALE).then_inc(S["wr_hi"], 1)

            for g in range(3):
                w_evac(0, g)
            u = 0
            for i in range(FT):
                for c, (n0, nn) in enumerate(NC3):
                    s.wait_ge(S["gu_mm"], u + 1)
                    if u >= 2:
                        s.wait_ge(S["hf_d"], u - 1)
                    s.activation(sg[:, u % 2, 0:nn], bank[2 * c][:, 0:nn], ACT.Silu, scale=1.0 / (W_SCALE * X_SCALE)).then_inc(S["sg_d"], 1)
                    s.wait_ge(S["hf_d"], u + 1)
                    s.activation(hT[:, 0, i, n0:n0 + nn], hf[:, u % 2, 0:nn], ACT.Copy).then_inc(S["h_hi"], 1)
                    u += 1
                    if i + 1 < FT:
                        w_evac(i + 1, c)

        @block.vector
        def _(v):
            n = [0]

            def own(ins):
                n[0] += 1
                ins.then_inc(S["v_own"], 1)
                v.wait_ge(S["v_own"], n[0])

            def counts_low(b):
                for c, (n0, nn) in enumerate(NC3):
                    v.wait_ge(S["cnt_hi"], 3 * b + c + 1)
                    v.tensor_tensor(counts[:, 1, b, n0:n0 + nn], bank[3 * (b % 2) + c][0:P, 0:nn], counts[:, 0, b, n0:n0 + nn], ALU.subtract).then_inc(S["cnt_lo"], 1)

            v.wait_ge(S["small_in"], 32)
            for t in range(NT):
                v.wait_ge(S["x_in"], 16 * NT)
                own(v.bn_stats(st6[:, t, :], xr[:, t, :]))
                v.bn_aggr(mv[:, t, :], st6[:, t, :]).then_inc(S["stats_v"], 1)
            v.wait_ge(S["gT_mm"], 1)
            v.tensor_scalar(gcol[:], bank[7][:, 0:K], W_SCALE, None, ALU.mult).then_inc(S["stats_v"], 1)
            v.wait_ge(S["stats_v"], NT + 1)
            for g in range(4):
                for k in range(K):
                    m = 4 * g + k
                    v.wait_ge(S["prep_hi"], m + 1)
                    if g < 3:
                        d = slice(g * D, (g + 1) * D)
                        v.scalar_tensor_tensor(wqkvT[:, 1, k, d], bank[m % 4][:, :], gcol[:, k:k + 1], wqkvT[:, 0, k, d], ALU.mult, ALU.subtract).then_inc(S["prep_lo"], 1)
                    else:
                        v.scalar_tensor_tensor(woutT[:, 1, k, :], bank[m % 4][:, :], W_SCALE, woutT[:, 0, k, :], ALU.mult, ALU.subtract).then_inc(S["prep_lo"], 1)
            for g in range(2):
                v.wait_ge(S["wcn_hi"], g + 1)
                d = slice(g * D, (g + 1) * D)
                v.scalar_tensor_tensor(wcn[:, 1, :, d], raw, W_SCALE, wcn[:, 0, :, d], ALU.mult, ALU.subtract).then_inc(S["wcn_lo"], 1)
            v.wait_ge(S["r_ready"], 1)

            def norm(t):
                if t >= 2:
                    v.wait_ge(S["xT_done"], t - 1)
                v.tensor_scalar(xn[:, t % 2, :], xr[:, t, :], mv[:, t, 0:1], rstd[:, t:t + 1], ALU.subtract, ALU.mult).then_inc(S["xn_ready"], 1)

            def xT_low(t):
                v.wait_ge(S["xT_hi"], t + 1)
                v.scalar_tensor_tensor(xT[:, t % 2, 1, :, :], bank[5][:, 0:K * P].rearrange("p (k n) -> p k n", k=K), X_SCALE, xT[:, t % 2, 0, :, :], ALU.mult, ALU.subtract).then_inc(S["xT_lo"], 1)

            def qT_low(t):
                v.wait_ge(S["qT_hi"], t + 1)
                d = slice(t * P, (t + 1) * P)
                v.scalar_tensor_tensor(qT[:, 1, :, d], bank[6][:, 0:K * P].rearrange("p (k n) -> p k n", k=K), Q_SCALE, qT[:, 0, :, d], ALU.mult, ALU.subtract).then_inc(S["qT_lo"], 1)

            heads = lambda ap: ap.rearrange("p (h d) -> p h d", d=HEAD)
            spread = lambda ap: ap.rearrange("p (h o) -> p h o", o=1).broadcast_to([P, HEADS, HEAD])
            norm(0)
            norm(1)
            xT_low(0)
            for t in range(NT):
                v.wait_ge(S["k_out"], t + 1)
                if t == 0:
                    own(v.tensor_copy(kmax[:], kf[:, 0, :]))
                    v.tensor_copy(kmax[:], kf[:, 0, :]).then_inc(S["kmax_d"], 1)
                else:
                    v.wait_ge(S["kmax_d"], t)
                    v.tensor_tensor(kmax[:], kmax[:], kf[:, t, :], ALU.max).then_inc(S["kmax_d"], 1)
                v.wait_ge(S["q_mm"], t + 1)
                v.tensor_reduce(qmx[:], heads(bank[3][0:P, :]), AX.X, ALU.max).then_inc(S["q_max"], 1)
                v.wait_ge(S["q_max"], t + 1)
                if t:
                    v.wait_ge(S["q_norm"], t)
                v.tensor_tensor(heads(qe[:]), heads(bank[3][0:P, :]), spread(qmx[:]), ALU.subtract).then_inc(S["q_sub"], 1)
                v.wait_ge(S["q_exp"], t + 1)
                v.tensor_reduce(qsum[:], heads(qe[:]), AX.X, ALU.add).then_inc(S["q_sum"], 1)
                v.wait_ge(S["q_sum"], t + 1)
                v.reciprocal(qsum[:], qsum[:]).then_inc(S["q_rec"], 1)
                v.wait_ge(S["q_rec"], t + 1)
                if t:
                    v.wait_ge(S["qT_mm"], t)
                v.tensor_tensor(heads(qn[:]), heads(qe[:]), spread(qsum[:]), ALU.mult).then_inc(S["q_norm"], 1)
                v.wait_ge(S["v_hi"], t + 1)
                v.scalar_tensor_tensor(vp[:, 1, t, :, 0:128], bank[2][0:P, :].rearrange("p (k e) -> p k e", k=K), r2v[:, t:t + 1], vp[:, 0, t, :, 0:128], ALU.mult, ALU.subtract).then_inc(S["v_lo"], 1)
                if t + 2 < NT:
                    norm(t + 2)
                if t + 1 < NT:
                    xT_low(t + 1)
                v.wait_ge(S["beta_hi"], t + 1)
                v.scalar_tensor_tensor(betas[:, 1, t, :], bank[0][0:P, :], 1.0 / W_SCALE, betas[:, 0, t, :], ALU.mult, ALU.subtract).then_inc(S["beta_lo"], 1)
                v.wait_ge(S["alpha_mm"], t + 1)
                v.wait_ge(S["xb_done"], t + 1)
                v.scalar_tensor_tensor(xr[:, t, :], bank[4][0:P, :], 1.0 / (W_SCALE * X_SCALE), xr[:, t, :], ALU.mult, ALU.add).then_inc(S["acc_done"], 1)
                qT_low(t)
            v.wait_ge(S["kmT_mm"], 1)
            v.tensor_reduce(kmaxc[:], bank[7][:, 0:K * P].rearrange("p (k n) -> p k n", k=K), AX.X, ALU.max).then_inc(S["kmc_d"], 1)
            v.wait_ge(S["kmb_mm"], 1)
            for t in range(NT):
                v.tensor_tensor(kf[:, t, :], kf[:, t, :], bank[7][0:P, :], ALU.subtract).then_inc(S["k_sub"], 1)
            v.wait_ge(S["ctx_mm"], 1)
            for k in range(K):
                own(v.reciprocal(krec[:, k:k + 1], bank[k][:, 128:129]))
                if k:
                    v.wait_ge(S["ctxT_mm"], k)
                v.tensor_scalar(ctxn[:], bank[k][:, 0:128], krec[:, k:k + 1], 1.0 / X_SCALE, ALU.mult, ALU.mult).then_inc(S["ctx_n"], 1)
                v.wait_ge(S["ctx_hi"], k + 1)
                for h in range(2):
                    d = slice(64 * h, 64 * h + 64)
                    i = v.scalar_tensor_tensor(ctxT[d, 1, d], bank[4][d, d], C_SCALE, ctxT[d, 0, d], ALU.mult, ALU.subtract)
                i.then_inc(S["ctx_lo"], 1)
                v.wait_ge(S["w2_hi"], k + 1)
                v.scalar_tensor_tensor(w2[:, 1, k, :], bank[5][:, :], 1.0 / W_SCALE, w2[:, 0, k, :], ALU.mult, ALU.subtract).then_inc(S["w2_lo"], 1)

            v.memset(edges_i, N).then_inc(S["fill_d"], 1)
            v.wait_ge(S["edge_in"], 64)
            own(v.tensor_copy(edges, edges_i))
            own(v.tensor_reduce(ext[:, 0:1], edges[:, 1, :], AX.X, ALU.max))
            own(v.tensor_reduce(ext[:, 1:2], edges[:, 1, :], AX.X, ALU.min))
            own(v.tensor_scalar(ov[:, 0, :], block_at[:], ext[:, 0:1], None, ALU.is_le))
            own(v.tensor_scalar(ext[:, 1:2], ext[:, 1:2], float(P - 1), None, ALU.subtract))
            own(v.tensor_scalar(ov[:, 1, :], block_at[:], ext[:, 1:2], None, ALU.is_ge))
            own(v.tensor_tensor(ov[:, 0, :], ov[:, 0, :], ov[:, 1, :], ALU.mult))
            own(v.tensor_scalar(ov[:, 2, :], ov[:, 0, :], group_no[:], None, ALU.mult))
            own(v.tensor_scalar(ext[:, 2:3], group_no[:], -1.0, float(NG + 1), ALU.mult, ALU.add))
            v.tensor_scalar(ov[:, 3, :], ov[:, 0, :], ext[:, 2:3], None, ALU.mult).then_inc(S["bound_v"], 1)
            v.wait_ge(S["bT_mm"], 1)
            own(v.tensor_reduce(bounds[:, 0:2], bank[6][0:NT, 0:2 * NG].rearrange("p (a j) -> p a j", a=2), AX.X, ALU.max))
            own(v.tensor_scalar(bounds[:, 0:1], bounds[:, 0:1], 3.0, None, ALU.max))
            own(v.tensor_scalar(bounds[:, 2:3], bounds[:, 0:1], -3.0, None, ALU.add))
            own(v.tensor_scalar(bounds[:, 1:2], bounds[:, 1:2], -1.0, float(NG), ALU.mult, ALU.add))
            v.tensor_tensor(bounds[:, 1:2], bounds[:, 1:2], bounds[:, 2:3], ALU.min).then_inc(S["bound_v"], 1)
            own(v.tensor_copy(eT.rearrange("p g q -> p q g"), bank[7][0:P, 0:8 * NG].rearrange("p (q g) -> p q g", g=NG)))
            v.wait_ge(S["bp_mm"], 1)
            v.tensor_copy(brow[:], bank[0][0:1, 0:2 * NT]).then_inc(S["brow_d"], 1)
            own(v.tensor_scalar(iota_b[:], iota_n[:, 0:P], float(P), None, ALU.subtract))
            v.wait_ge(S["brow_d"], 1)
            visit = v.alloc_register("dve_visit")
            v.reg_mov(visit, 0)
            for b in range(NT):
                v.tensor_scalar(iota_b[:], iota_b[:], float(P), None, ALU.add).then_inc(S["iota_d"], 1)
                v.wait_ge(S["iota_d"], b + 1)
                hi = v.value_load(brow[0:1, b:b + 1], min_val=3, max_val=NG)
                lo = v.value_load(brow[0:1, b + NT:b + NT + 1], min_val=0, max_val=NG - 3)
                with v.Fori(lo, hi) as j:
                    w = v.snap(visit, min_val=0, max_val=NT * NG * GRP)
                    for q in range(GRP):
                        v.wait_ge(S["oh_used"], w + (q + 1))
                        v.tensor_scalar(oh_src[:, q, :], iota_n[:], eT[:, bass.ds(j, 1), 2 * q].rearrange("p a -> p a"), None, ALU.is_equal)
                        v.tensor_scalar(oh_dst[:, q, 0:P], iota_b[:], eT[:, bass.ds(j, 1), 2 * q + 1].rearrange("p a -> p a"), None, ALU.is_equal).then_inc(S["oh_ready"], 1)
                    v.reg_add(visit, visit, GRP)
                if b:
                    counts_low(b - 1)
            counts_low(NT - 1)
            for t in range(NT):
                v.wait_ge(S["cn_mm"], t + 1)
                v.reciprocal(stat[:, 6:7], bank[4 + t % 2][0:P, 0:1]).then_inc(S["crec_d"], 1)
                v.wait_ge(S["crec_d"], t + 1)
                own(v.tensor_scalar(stat[:, 6:7], stat[:, 6:7], 1.0 / X_SCALE, None, ALU.mult))
                own(v.bn_stats(st6[:, 0, :], bank[2 + t % 2][0:P, :]))
                v.bn_aggr(stat[:, 4:6], st6[:, 0, :]).then_inc(S["mst_v"], 1)
                v.scalar_tensor_tensor(xr[:, t, :], bank[t % 2][0:P, :], stat[:, 6:7], xr[:, t, :], ALU.mult, ALU.add).then_inc(S["gam_d"], 1)
                v.wait_ge(S["mst_p"], t + 1)
                own(v.tensor_scalar(stat[:, 2:3], stat[:, 1:2], MIX, None, ALU.mult))
                v.scalar_tensor_tensor(stat[:, 3:4], stat[:, 4:5], -1.0, stat[:, 2:3], ALU.mult, ALU.mult).then_inc(S["mst_w"], 1)
                v.wait_ge(S["mix_g"], t + 1)
                v.wait_ge(S["gam_d"], t + 1)
                v.tensor_tensor(xr[:, t, :], xr[:, t, :], xn[:, 0, :], ALU.add).then_inc(S["x1_d"], 1)
                v.wait_ge(S["x1_d"], t + 1)
                own(v.bn_stats(st6[:, 1, :], xr[:, t, :]))
                v.bn_aggr(stat[:, 12:14], st6[:, 1, :]).then_inc(S["x1_st"], 1)
                v.wait_ge(S["x1_p"], t + 1)
                if t:
                    v.wait_ge(S["x2T_mm"], t)
                v.tensor_scalar(xn[:, 1, :], xr[:, t, :], stat[:, 12:13], stat[:, 9:10], ALU.subtract, ALU.mult).then_inc(S["x2_n"], 1)
                v.wait_ge(S["x2_hi"], t + 1)
                d = slice(t * P, (t + 1) * P)
                v.scalar_tensor_tensor(qT[:, 1, :, d], bank[6][:, 0:K * P].rearrange("p (k n) -> p k n", k=K), X_SCALE, qT[:, 0, :, d], ALU.mult, ALU.subtract).then_inc(S["x2_lo"], 1)

            def quantise(i):
                v.wait_ge(S[f"wr_in{i % 2}"], 48 * (i // 2 + 1))
                v.tensor_reduce(gsum[:, 0, :], wraw[:, i % 2, :, :], AX.X, ALU.add, apply_absolute_value=True).then_inc(S["wr_abs"], 1)
                v.wait_ge(S["wr_abs"], i + 1)
                if i:
                    v.wait_ge(S["wr_b"], i)
                own(v.tensor_scalar(gthr[:, 0, :], gsum[:, 0, :], 1.0 / 128, EPS, ALU.mult, ALU.add))
                own(v.tensor_scalar(gthr[:, 1, :], gthr[:, 0, :], 0.5, None, ALU.mult))
                v.tensor_scalar(gthr[:, 2, :], gthr[:, 0, :], -0.5, None, ALU.mult).then_inc(S["wr_thr"], 1)
                if i >= 2:
                    v.wait_ge(S["wr_T"], 3 * (i - 1))
                for j in range(12):
                    ins = v.tensor_scalar(wa[:, i % 2, j, :], wraw[:, i % 2, j, :], gthr[:, 1, j:j + 1], gthr[:, 0, j:j + 1], ALU.is_gt, ALU.mult)
                ins.then_inc(S["wr_a"], 1)

            def w_low(i, g):
                v.wait_ge(S["wr_hi"], 3 * i + g + 1)
                b = bank[6 + (3 * i + g) % 2][:, :]
                if g < 2:
                    d = slice(g * D, (g + 1) * D)
                    v.scalar_tensor_tensor(wgu[:, i % 2, 1, d], b, W_SCALE, wgu[:, i % 2, 0, d], ALU.mult, ALU.subtract).then_inc(S["wr_lo"], 1)
                else:
                    v.scalar_tensor_tensor(wdT[:, 1, i, :], b, W_SCALE, wdT[:, 0, i, :], ALU.mult, ALU.subtract).then_inc(S["wr_lo"], 1)

            quantise(0)
            quantise(1)
            for g in range(3):
                w_low(0, g)
            u = 0
            for i in range(FT):
                if i + 2 < FT:
                    quantise(i + 2)
                for c, (n0, nn) in enumerate(NC3):
                    v.wait_ge(S["sg_d"], u + 1)
                    if u >= 2:
                        v.wait_ge(S["h_hi"], u - 1)
                    v.scalar_tensor_tensor(hf[:, u % 2, 0:nn], bank[2 * c + 1][:, 0:nn], H_SCALE / (W_SCALE * X_SCALE), sg[:, u % 2, 0:nn], ALU.mult, ALU.mult).then_inc(S["hf_d"], 1)
                    v.wait_ge(S["h_hi"], u + 1)
                    v.tensor_tensor(hT[:, 1, i, n0:n0 + nn], hf[:, u % 2, 0:nn], hT[:, 0, i, n0:n0 + nn], ALU.subtract).then_inc(S["h_lo"], 1)
                    u += 1
                    if i + 1 < FT:
                        w_low(i + 1, c)
            for t in range(NT):
                v.wait_ge(S["dn_mm"], t + 1)
                v.scalar_tensor_tensor(xr[:, t, :], bank[t % 2][0:P, :], 1.0 / (W_SCALE * H_SCALE), xr[:, t, :], ALU.mult, ALU.add).then_inc(S["dn_d"], 1)


_INS = ["x", "src", "dst", "L0_gnn_wc", "L0_gnn_wn", "L0_gnn_bias", "L0_mix_norm_gamma", "L0_mix_w_qkv", "L0_mix_w_out",
        "L0_mix_out_gamma", "L0_ffn_w_gate", "L0_ffn_w_up", "L0_ffn_w_down"]


def kernel(**inputs):
    import numpy as np
    import concourse.bacc as bacc
    import concourse.bass_utils as bass_utils

    nc = bacc.Bacc("TRN2", target_bir_lowering=False, num_devices=1)
    arrays, args = {}, []
    for name in _INS:
        a = np.ascontiguousarray(inputs[name])
        arrays[f"in_{name}"] = a
        args.append(nc.dram_tensor(f"in_{name}", a.shape, mybir.dt.from_np(a.dtype), kind="ExternalInput").ap())
    out = nc.dram_tensor("out", inputs["x"].shape, F32, kind="ExternalOutput").ap()
    gps_layer(nc, *args, out)
    return bass_utils.run_bass_kernel_spmd(nc, [arrays], core_ids=[0]).results[0]["out"]
```

```python
from contextlib import ExitStack

import concourse.bass as bass
from concourse import mybir

F32 = mybir.dt.float32
F16 = mybir.dt.float16
I32 = mybir.dt.int32
F8 = mybir.dt.float8e4
ALU = mybir.AluOpType
ACT = mybir.ActivationFunctionType
AX = mybir.AxisListType

EPS = 1e-5
W_SCALE = 64.0
X_SCALE = 32.0
Q_SCALE = 64.0
C_SCALE = 256.0
H_SCALE = 16.0
HEAD = 64
PARTS = ((0, 0), (1, 0), (0, 1))


def gps_layer(nc, x, src, dst, wc, wn, bias, g_norm, w_qkv, w_out, g_out, w_gate, w_up, w_down, out):
    N, D = x.shape
    E, = src.shape
    F = w_gate.shape[0]
    P = 125
    NT = N // P
    NCH = E // P
    ROWS = NCH // 2
    GRP = 4
    LEAST = 2 * GRP + 1
    K = D // 128
    FT = F // 128
    HEADS = D // HEAD
    NC3 = [(0, 417), (417, 417), (834, 416)]
    TILES_OF = [-(-(a + n) // P) for a, n in NC3]
    MIX = 1.0 / (Q_SCALE * C_SCALE * HEAD ** 0.5)
    UNDO = 1.0 / (W_SCALE * X_SCALE)
    assert N == NT * P and E == 2 * ROWS * P and D == 512 and w_qkv.shape[0] == 3 * D and F == FT * 128
    assert ROWS <= 128 and P + HEAD <= 512

    with ExitStack() as ctx:
        def sb(name, shape, dt):
            return ctx.enter_context(nc.sbuf_tensor(name, shape, dt))

        def sem(name):
            return ctx.enter_context(nc.semaphore(name))

        bank = [ctx.enter_context(nc.psum_tensor(f"bank{i}", [128, 512], F32)) for i in range(8)]

        ident = sb("ident", [128, 128], F32)
        iota_n = sb("iota_n", [P, N], F16)
        iota_b = sb("iota_b", [P, P], F16)
        block_at = sb("block_at", [ROWS, NT], F32)
        chunk_up = sb("chunk_up", [ROWS, 2], F32)
        chunk_dn = sb("chunk_dn", [ROWS, 2], F32)
        ones_h = sb("ones_h", [P, 1], F16)
        halfpow = sb("halfpow", [P, NT], F32)
        rows_b = sb("rows_b", [P, D], F32)
        grow = sb("grow", [K, 128], F32)
        gcol = sb("gcol", [128, K], F32)
        st6 = sb("st6", [P, NT, 6], F32)
        st6x = sb("st6x", [P, NT, 6], F32)
        mv = sb("mv", [P, NT, 2], F32)
        rstd = sb("rstd", [P, NT], F32)
        nvar = sb("nvar", [P, NT], F32)
        r2k = sb("r2k", [P, NT], F32)
        r2v = sb("r2v", [P, NT], F32)
        qmx = sb("qmx", [P, HEADS], F32)
        qsum = sb("qsum", [P, HEADS], F32)
        kmaxc = sb("kmaxc", [128, K], F32)
        krec = sb("krec", [128, K], F32)
        crec = sb("crec", [P, NT], F32)
        indeg = sb("indeg", [P, 3 * NT + 1], F32)
        flag_f = sb("flag_f", [1, 1], F32)
        flag = sb("flag", [1, 1], I32)
        mst = sb("mst", [P, 2, 6], F32)
        xst = sb("xst", [P, 2, 4], F32)
        ext = sb("ext", [ROWS, 2, 2], F32)
        bounds = sb("bounds", [NT, 3], F32)
        brow = sb("brow", [1, 2 * NT], I32)
        gsum = sb("gsum", [128, 12], F32)
        gthr = sb("gthr", [128, 3, 12], F32)
        xr = sb("xr", [P, NT, D], F32)
        betas = sb("betas", [P, 2, NT, D], F16)
        qT = sb("qT", [128, 2, K, NT * P], F16)
        xn = sb("xn", [P, 2, D], F32)
        small = sb("small", [128, 2704], F32)
        zone = sb("zone", [128, 31984], F32)

        def view(at, shape, dt, zone=zone):
            n = 1
            for s in shape[1:]:
                n *= s
            words = {F32: n, I32: n, F16: n // 2, F8: n // 4}[dt]
            v = zone[0:shape[0], at:at + words]
            if dt != F32:
                v = v.bitcast(dt)
            names = "abcd"[:len(shape) - 1]
            if len(shape) > 2:
                v = v.rearrange(f"p ({' '.join(names)}) -> p {' '.join(names)}", **{c: s for c, s in zip(names, shape[1:])})
            return v

        AT_OUT, AT_CN, AT_QKV, AT_KV = 9376, 11424, 15520, 21664
        counts = view(0, [P, NT, N], F16)
        counts_lo = view(6250, [P, NT, N], F8)
        woutT = view(AT_OUT, [128, 2, K, D], F16)
        wcn = view(AT_CN, [128, 2, K, 2 * D], F16)
        wqkvT = view(AT_QKV, [128, 2, K, 3 * D], F16)
        kf = view(AT_KV, [P, NT, D], F32)
        ek = view(AT_KV, [P, NT, 2, D], F16)
        vp = view(AT_KV + 5120, [P, 2, NT, K, 130], F16)
        raw = view(AT_KV, [128, 2, K, D], F32)
        stage_w = view(AT_KV + 4096, [128, 2, D], F32)
        stage_c = view(AT_KV + 5120, [P, N], F32)
        oh_src = view(AT_KV + 6370, [P, GRP, N], F16)
        oh_dst = view(AT_KV + 8870, [P, GRP, 128], F16)
        eT = view(AT_KV + 9126, [P, NCH + 3 * GRP, 2], F32)
        edges_i = view(0, [ROWS, 2, 2 * P], I32, small)
        edges = view(500, [ROWS, 2, 2, P], F32, small)
        ov = view(1000, [ROWS, 2, 4, NT], F32, small)
        qe = view(0, [P, D], F32, small)
        qn = view(512, [P, D], F32, small)
        ering = view(0, [P, 2, D], F32, small)
        xT = view(1024, [128, 2, 2, K, P], F16, small)
        kmax = view(2040, [P, D], F32, small)
        w2 = view(AT_CN, [128, 2, K, D], F16)
        ctxn = view(AT_CN + 2048, [128, 2, 128], F32)
        ctxT = view(AT_CN + 2304, [128, 2, 2, 128], F16)
        xn2 = view(0, [P, 2, D], F32, small)
        sg = view(1024, [128, 2, 417], F32, small)
        hf = view(1860, [128, 2, 417], F32, small)
        wraw = view(AT_QKV, [128, 2, 12, 128], F32)
        wa = view(AT_QKV + 3072, [128, 2, 12, 128], F32)
        wb = view(AT_KV, [128, 12, 128], F32)
        wgu = view(AT_KV + 1536, [128, 2, 2, 2 * K * 128], F16)
        wdT = view(AT_KV + 3584, [128, 2, FT, D], F16)
        hT = view(0, [128, 2, FT, N], F16)

        S = {}

        def sems(text):
            for n in text.split():
                S[n] = sem(n)

        sems("""v_own p_own edge_in small_in gain_in x_in0 x_in1 x_in2 x_in3 x_in4 raw_in0 raw_in1 wr_in0 wr_in1
            g_ident g_const stats_v gcol_d r_ready gT_mm
            edge_f bound_v bT_mm bp_mm brow_d iota_d oh_ready oh_used cnt_mm cnt_out cnt_lo
            prep_T prep_out prep_lo wcn_own wcn_hi wcn_lo flag_c flag_mm flag_d cn_mm crec_d
            xn_ready xT_done xT_hi xT_lo beta_mm k_mm v_mm q_mm alpha_mm
            beta_hi beta_lo k_out kmax_d v_hi v_lo q_max q_sub q_exp q_sum q_rec q_norm qT_mm qT_hi qT_lo
            xb_done acc_done kmT_mm kmc_d kmb_mm k_sub k_exp ek_hi ek_lo v_one ctx_mm ctx_n ctxT_mm
            ctx_zero ctx_hi ctx_lo w2_mm w2_hi w2_lo gam_mm gam_d mix_mm mst_v mst_p mix_n mix_g x1_d x1_st x1_p x2_n
            x2T_mm x2_hi x2_lo wr_abs wr_thr wr_a wr_b wr_q wr_T wr_hi wr_lo gu_mm sg_d hf_d h_hi h_lo dn_mm dn_d
            out_0 out_1""")

        def tiles(b):
            return b[:, 0:K * P].rearrange("p (k n) -> p k n", k=K)

        block = ctx.enter_context(nc.Block())

        @block.sync
        def _(sp):
            for a, e in enumerate((src, dst)):
                sp.dma_start(edges_i[:, a, :], e.rearrange("(r e) -> r e", e=2 * P)).then_inc(S["edge_in"], 16)
            sp.dma_start(grow[:], g_norm.rearrange("(k p) -> k p", p=128)).then_inc(S["small_in"], 16)
            sp.dma_start(rows_b[:], bias.rearrange("(a d) -> a d", a=1).broadcast_to([P, D])).then_inc(S["small_in"], 16)

            def load_raw(n):
                if n >= 2:
                    sp.wait_ge(S["prep_T"], 4 * (n - 1))
                w = [w_qkv[0:D, :], w_qkv[D:2 * D, :], w_qkv[2 * D:3 * D, :], w_out, wc, wn][n]
                sp.dma_start(raw[:, n % 2, :, :], w.rearrange("(j p) c -> p j c", p=128)).then_inc(S[f"raw_in{n % 2}"], 16)

            load_raw(0)
            for t in range(0, NT, 2):
                sp.dma_start(xr[:, t:t + 2, :], x[t * P:(t + 2) * P, :].rearrange("(t p) d -> p t d", p=P)).then_inc(S[f"x_in{t // 2}"], 16)
            for n in range(1, 6):
                load_raw(n)
            sp.wait_ge(S["xb_done"], NT)
            sp.dma_start(rows_b[:], g_out.rearrange("(a d) -> a d", a=1).broadcast_to([P, D])).then_inc(S["gain_in"], 16)
            sp.wait_ge(S["v_mm"], NT)
            for i in range(FT):
                if i >= 2:
                    sp.wait_ge(S["wr_a"], i - 1)
                    sp.wait_ge(S["wr_b"], i - 1)
                f = slice(i * 128, (i + 1) * 128)
                into = wraw[:, i % 2, :, :]
                done = S[f"wr_in{i % 2}"]
                sp.dma_start(into[:, 0:4, :], w_gate[f, :].rearrange("p (k d) -> p k d", d=128)).then_inc(done, 16)
                sp.dma_start(into[:, 4:8, :], w_up[f, :].rearrange("p (k d) -> p k d", d=128)).then_inc(done, 16)
                sp.dma_start(into[:, 8:12, :], w_down[:, f].rearrange("(k p) d -> p k d", p=128)).then_inc(done, 16)
            for t in range(NT):
                sp.wait_ge(S["dn_d"], t + 1)
                sp.dma_start(out[t * P:(t + 1) * P, :], xr[:, t, :]).then_inc(S[f"out_{t % 2}"], 16)
            for h in range(2):
                sp.wait_ge(S[f"out_{h}"], 16 * NT // 2)

        @block.gpsimd
        def _(g):
            n_own = [0]

            def own(ins):
                n_own[0] += 1
                ins.then_inc(S["p_own"], 1)
                g.wait_ge(S["p_own"], n_own[0])

            def iota(out, pattern, base, mult):
                g.iota(out, pattern, base=base, channel_multiplier=mult, allow_small_or_imprecise_dtypes=True).then_inc(S["g_const"], 1)

            iota(block_at[:], [[P, NT]], 0, 0)
            iota(chunk_up[:], [[1, 2]], 1, 2)
            iota(chunk_dn[:], [[-1, 2]], NCH, -2)
            g.memset(ident[:], 0.0).then_inc(S["g_ident"], 1)
            g.wait_ge(S["g_ident"], 1)
            g.affine_select(out=ident[:], in_=ident[:], compare_op=ALU.not_equal, fill=1.0, base=0,
                            pattern=[[-1, 128]], channel_multiplier=1).then_inc(S["g_ident"], 1)
            iota(iota_n[:], [[1, N]], 0, 0)
            g.memset(eT[:, NCH:NCH + 3 * GRP, :], float(N)).then_inc(S["g_const"], 1)
            g.memset(ones_h[:], 1.0).then_inc(S["g_const"], 1)
            g.memset(halfpow[:], -0.5).then_inc(S["g_const"], 1)
            g.wait_ge(S["g_const"], 7)

            def prep_low(n):
                g.wait_ge(S["prep_out"], n + 1)
                to, k = (wqkvT, n % K) if n < 3 * K else (woutT, n % K)
                d = slice((n // K) * D, (n // K + 1) * D) if n < 3 * K else slice(0, D)
                g.tensor_tensor(to[:, 1, k, d], stage_w[:, n % 2, :], to[:, 0, k, d], ALU.subtract).then_inc(S["prep_lo"], 1)

            def counts_low(b):
                g.wait_ge(S["cnt_out"], 3 * (b + 1))
                g.tensor_tensor(counts_lo[:, b, :], stage_c, counts[:, b, :], ALU.subtract, saturate=False).then_inc(S["cnt_lo"], 1)

            for b in range(NT):
                if b >= 1 and 2 * (b - 1) + 1 < 4 * K:
                    prep_low(2 * b - 2)
                    prep_low(2 * b - 1)
                if b == 6:
                    g.wait_ge(S["stats_v"], NT)
                    own(g.tensor_scalar(nvar[:], mv[:, :, 1], EPS, None, ALU.add))
                    own(g.tensor_tensor(rstd[:], nvar[:], halfpow[:], ALU.pow))
                    own(g.tensor_tensor(nvar[:], rstd[:], rstd[:], ALU.mult))
                    own(g.tensor_tensor(nvar[:], nvar[:], mv[:, :, 1], ALU.mult))
                    own(g.tensor_scalar(nvar[:], nvar[:], EPS, None, ALU.add))
                    own(g.tensor_tensor(r2k[:], nvar[:], halfpow[:], ALU.pow))
                    own(g.tensor_scalar(r2v[:], r2k[:], X_SCALE * UNDO, None, ALU.mult))
                    g.tensor_scalar(r2k[:], r2k[:], UNDO, None, ALU.mult).then_inc(S["r_ready"], 1)
                if b >= 1:
                    counts_low(b - 1)
            for i in range(2):
                g.wait_ge(S["wcn_hi"], i + 1)
                g.tensor_tensor(wcn[:, 1, :, i * D:(i + 1) * D], raw[:, i % 2, :, :], wcn[:, 0, :, i * D:(i + 1) * D], ALU.subtract).then_inc(S["wcn_lo"], 1)
            counts_low(NT - 1)
            g.wait_ge(S["cnt_lo"], NT)
            for h in range(2):
                g.memset(vp[:, h, :, :, 128:129].rearrange("p t k o -> p (t k) o"), 1.0 - h).then_inc(S["v_one"], 1)
            g.wait_ge(S["small_in"], 32)
            for t in range(NT):
                g.wait_ge(S["xn_ready"], t + 1)
                g.tensor_tensor(xr[:, t, :], xr[:, t, :], rows_b[:], ALU.add).then_inc(S["xb_done"], 1)
            for t in range(NT):
                g.wait_ge(S["ek_hi"], t + 1)
                g.tensor_tensor(ek[:, t, 1, :], ering[:, t % 2, :], ek[:, t, 0, :], ALU.subtract).then_inc(S["ek_lo"], 1)
            g.wait_ge(S["beta_mm"], NT)
            g.wait_ge(S["alpha_mm"], NT)
            g.memset(ctxT, 0.0).then_inc(S["ctx_zero"], 1)
            g.wait_ge(S["gain_in"], 16)

            def mix_stats(t):
                m = mst[:, t % 2, :]
                g.wait_ge(S["mst_v"], t + 1)
                if t >= 2:
                    g.wait_ge(S["mix_n"], t - 1)
                own(g.tensor_scalar(m[:, 2:3], m[:, 1:2], MIX * MIX, EPS, ALU.mult, ALU.add))
                own(g.tensor_tensor(m[:, 3:4], m[:, 2:3], halfpow[:, 0:1], ALU.pow))
                own(g.tensor_scalar(m[:, 4:5], m[:, 3:4], MIX, None, ALU.mult))
                own(g.tensor_scalar(m[:, 5:6], m[:, 0:1], -1.0, None, ALU.mult))
                g.tensor_tensor(m[:, 5:6], m[:, 5:6], m[:, 4:5], ALU.mult).then_inc(S["mst_p"], 1)

            def mix_gain(t):
                g.wait_ge(S["mix_n"], t + 1)
                g.tensor_tensor(xn[:, t % 2, :], xn[:, t % 2, :], rows_b[:], ALU.mult).then_inc(S["mix_g"], 1)

            def x1_stats(t):
                m = xst[:, t % 2, :]
                g.wait_ge(S["x1_st"], t + 1)
                own(g.tensor_scalar(m[:, 2:3], m[:, 1:2], EPS, None, ALU.add))
                g.tensor_tensor(m[:, 3:4], m[:, 2:3], halfpow[:, 0:1], ALU.pow).then_inc(S["x1_p"], 1)

            def quantise_low(i):
                g.wait_ge(S["wr_thr"], i + 1)
                g.wait_ge(S[f"wr_in{i % 2}"], 48 * (i // 2 + 1))
                if i:
                    g.wait_ge(S["wr_q"], i)
                for j in range(12):
                    ins = g.tensor_scalar(wb[:, j, :], wraw[:, i % 2, j, :], gthr[:, 2, j:j + 1], gthr[:, 0, j:j + 1], ALU.is_lt, ALU.mult)
                ins.then_inc(S["wr_b"], 1)
                g.wait_ge(S["wr_b"], i + 1)
                g.wait_ge(S["wr_a"], i + 1)
                g.tensor_tensor(wa[:, i % 2, :, :], wa[:, i % 2, :, :], wb, ALU.subtract).then_inc(S["wr_q"], 1)

            for t in range(NT + 1):
                if t < NT:
                    mix_stats(t)
                    mix_gain(t)
                if t:
                    x1_stats(t - 1)
                if t == 4:
                    quantise_low(0)
                if t == 7:
                    quantise_low(1)
            for i in range(2, FT):
                quantise_low(i)

        @block.tensor
        def _(pe):
            def triple(to, stat, mov, pairs, first=True, last=True):
                n, total = 0, 3 * len(pairs)
                for p in pairs:
                    for a, m in PARTS:
                        ins = pe.matmul(to, stat(a, p), mov(m, p), start=first and n == 0, stop=last and n == total - 1)
                        n += 1
                return ins

            def turn_x(t):
                pe.wait_ge(S["xn_ready"], t + 1)
                if t:
                    pe.wait_ge(S["xT_lo"], t)
                for k in range(K):
                    ins = pe.transpose(bank[6 if t == 0 else 5][:, k * P:(k + 1) * P], xn[:, t % 2, k * 128:(k + 1) * 128], ident[0:P, 0:P])
                ins.then_inc(S["xT_done"], 1)

            pe.wait_ge(S["g_ident"], 2)
            pe.wait_ge(S["edge_f"], 1)
            for h in range(2):
                for a in range(2):
                    ins = pe.transpose(bank[7 - h][0:P, a * ROWS:(a + 1) * ROWS], edges[:, a, h, :], ident[0:ROWS, 0:ROWS])
            ins.then_inc(S["bT_mm"], 1)
            pe.wait_ge(S["bound_v"], 1)
            for a in range(2):
                for h in range(2):
                    at = (a * 2 + h) * ROWS
                    ins = pe.transpose(bank[0][0:NT, at:at + ROWS], ov[:, h, 2 + a, :], ident[0:ROWS, 0:ROWS])
            ins.then_inc(S["bT_mm"], 1)
            pe.wait_ge(S["bound_v"], 2)
            for a in range(2):
                ins = pe.transpose(bank[1][0:1, a * NT:(a + 1) * NT], bounds[:, a:a + 1], ident[0:NT, 0:NT])
            ins.then_inc(S["bp_mm"], 1)
            pe.wait_ge(S["small_in"], 32)
            pe.transpose(bank[2][:, 0:K], grow[:], ident[0:K, 0:K]).then_inc(S["gT_mm"], 1)
            pe.wait_ge(S["brow_d"], 1)
            pe.wait_ge(S["gcol_d"], 1)
            pe.nop().then_inc(S["oh_used"], GRP)
            visit = pe.alloc_register("pe_visit")
            pe.reg_mov(visit, 0)

            def prep(n):
                pe.wait_ge(S[f"raw_in{n // K % 2}"], 16 * (n // K // 2 + 1))
                if n >= 2:
                    pe.wait_ge(S["prep_out"], n - 1)
                for j in range(4):
                    ins = pe.transpose(bank[6 + n % 2][:, j * 128:(j + 1) * 128], raw[:, n // K % 2, j, n % K * 128:(n % K + 1) * 128], ident[:])
                ins.then_inc(S["prep_T"], 1)

            for b in range(NT):
                if b >= 2:
                    pe.wait_ge(S["cnt_out"], 3 * (b - 1))
                hi = pe.value_load(brow[0:1, b:b + 1], min_val=LEAST, max_val=NCH + LEAST)
                lo = pe.value_load(brow[0:1, b + NT:b + NT + 1], min_val=0, max_val=NCH)

                def group(first, last):
                    w = pe.snap(visit, min_val=0, max_val=NT * (NCH + 3 * GRP))
                    for q in range(GRP):
                        pe.wait_ge(S["oh_ready"], w + (q + 1))
                        for c, (n0, nn) in enumerate(NC3):
                            ins = pe.matmul(bank[3 * (b % 2) + c][0:P, 0:nn], oh_dst[:, q, 0:P], oh_src[:, q, n0:n0 + nn],
                                            start=first and q == 0, stop=True, skip_group_check=True)
                        ins.then_inc(S["oh_used"], 1)
                        if last and q == GRP - 1:
                            pe.matmul(bank[3 * (b % 2) + 2][0:1, 511:512], ones_h[:], ones_h[:], start=False, stop=True, skip_group_check=True).then_inc(S["cnt_mm"], 1)
                    pe.reg_add(visit, visit, GRP)

                group(True, False)
                with pe.Fori(lo + GRP, hi - GRP, GRP):
                    group(False, False)
                if b < 2 * K:
                    prep(2 * b)
                    prep(2 * b + 1)
                if b == NT - 1:
                    turn_x(0)
                group(False, True)

            def product(b, t, w, c0, done):
                triple(b[0:P, :], lambda a, k: xT[:, t % 2, a, k, :], lambda m, k: w[:, m, k, c0:c0 + D], range(K)).then_inc(done, 1)

            def turn_q(t):
                pe.wait_ge(S["q_norm"], t + 1)
                if t:
                    pe.wait_ge(S["qT_lo"], t)
                for k in range(K):
                    ins = pe.transpose(bank[6][:, k * P:(k + 1) * P], qn[:, k * 128:(k + 1) * 128], ident[0:P, 0:P])
                ins.then_inc(S["qT_mm"], 1)

            pe.wait_ge(S["prep_lo"], 4 * K)
            pe.wait_ge(S["cnt_out"], 3 * NT)
            over = None
            for t in range(NT):
                pe.wait_ge(S["xT_lo"], t + 1)
                if t:
                    pe.wait_ge(S["k_out"], t)
                product(bank[1], t, wqkvT, D, S["k_mm"])
                if t:
                    pe.wait_ge(S["q_sub"], t)
                product(bank[3], t, wqkvT, 0, S["q_mm"])
                if t:
                    turn_q(t - 1)
                    pe.wait_ge(S["v_lo"], t)
                product(bank[2], t, wqkvT, 2 * D, S["v_mm"])
                if t + 1 < NT:
                    turn_x(t + 1)
                if t == 1:
                    pe.wait_ge(S["flag_c"], 1)
                    pe.transpose(bank[7][0:1, 0:P], indeg[:, 3 * NT:3 * NT + 1], ident[0:P, 0:P]).then_inc(S["flag_mm"], 1)
                if t == 3:
                    pe.wait_ge(S["flag_d"], 1)
                    over = pe.value_load(flag[0:1, 0:1], min_val=0, max_val=1)
                    pe.wait_ge(S["cnt_lo"], NT)
                    for u in range(NT):
                        for m in range(NT - 1):
                            pe.matmul(bank[7][0:P, u:u + 1], counts[:, m, u * P:(u + 1) * P], ones_h[:], start=m == 0, stop=False, skip_group_check=True)
                        with pe.If(over):
                            for m in range(NT):
                                pe.matmul(bank[7][0:P, u:u + 1], counts_lo[:, m, u * P:(u + 1) * P], ones_h[:], start=False, stop=False, skip_group_check=True)
                        ins = pe.matmul(bank[7][0:P, u:u + 1], counts[:, NT - 1, u * P:(u + 1) * P], ones_h[:], start=False, stop=True, skip_group_check=True)
                    ins.then_inc(S["cn_mm"], 1)
                if t == NT - 1:
                    pe.wait_ge(S["crec_d"], 1)
                    pe.wait_ge(S["kmax_d"], NT)
                    for k in range(K):
                        ins = pe.transpose(bank[7][:, k * P:(k + 1) * P], kmax[:, k * 128:(k + 1) * 128], ident[0:P, 0:P])
                    ins.then_inc(S["kmT_mm"], 1)
                if t:
                    pe.wait_ge(S["beta_lo"], t)
                else:
                    pe.wait_ge(S["wcn_lo"], 2)
                product(bank[0], t, wcn, D, S["beta_mm"])
                if t:
                    pe.wait_ge(S["acc_done"], t)
                product(bank[4], t, wcn, 0, S["alpha_mm"])
            pe.wait_ge(S["kmc_d"], 1)
            for k in range(K):
                ins = pe.matmul(bank[7][0:P, k * 128:(k + 1) * 128], kmaxc[:, k:k + 1].broadcast_to([128, P]), ident[:], start=True, stop=True)
            ins.then_inc(S["kmb_mm"], 1)
            turn_q(NT - 1)

            def gamma(t):
                if t >= 2:
                    pe.wait_ge(S["gam_d"], t - 1)
                to = bank[t % 2][0:P, :]
                for m in range(NT):
                    for c in range(2):
                        if m == NT - 1 and c == 1:
                            with pe.If(over):
                                for o in range(NT):
                                    pe.matmul(to, counts_lo[:, o, t * P:(t + 1) * P], betas[:, 0, o, :], start=False, stop=False)
                        ins = pe.matmul(to, counts[:, m, t * P:(t + 1) * P], betas[:, c, m, :], start=m == 0 and c == 0, stop=m == NT - 1 and c == 1)
                ins.then_inc(S["gam_mm"], 1)

            def mix(t):
                if t >= 2:
                    pe.wait_ge(S["mix_n"], t - 1)
                triple(bank[2 + t % 2][0:P, :], lambda a, k: qT[:, a, k, t * P:(t + 1) * P], lambda m, k: w2[:, m, k, :], range(K)).then_inc(S["mix_mm"], 1)

            def turn_x1(t):
                pe.wait_ge(S["x2_n"], t + 1)
                if t >= 2:
                    pe.wait_ge(S["x2_lo"], t - 1)
                for k in range(K):
                    ins = pe.transpose(bank[4 + t % 2][:, k * P:(k + 1) * P], xn2[:, t % 2, k * 128:(k + 1) * 128], ident[0:P, 0:P])
                ins.then_inc(S["x2T_mm"], 1)

            pe.wait_ge(S["beta_lo"], NT)
            for t in range(3):
                gamma(t)
            pe.wait_ge(S["v_one"], 2)
            pe.wait_ge(S["v_lo"], NT)
            pe.wait_ge(S["q_sub"], NT)
            pe.wait_ge(S["acc_done"], NT)
            for t in range(NT):
                pe.wait_ge(S["ek_lo"], t + 1)
                for k in range(K):
                    ins = triple(bank[2 + k][:, 0:129], lambda a, p: ek[:, t, a, k * 128:(k + 1) * 128], lambda m, p: vp[:, m, t, k, 0:129],
                                 [0], t == 0, t == NT - 1)
            ins.then_inc(S["ctx_mm"], 1)
            gamma(3)
            pe.wait_ge(S["qT_lo"], NT)
            pe.wait_ge(S["k_sub"], NT)
            for k in range(K):
                pe.wait_ge(S["ctx_n"], k + 1)
                pe.transpose(bank[6][:, 0:128], ctxn[:, k % 2, :], ident[:]).then_inc(S["ctxT_mm"], 1)
                gamma(4 + k)
                pe.wait_ge(S["ctx_lo"], k + 1)
                if k:
                    pe.wait_ge(S["w2_lo"], k)
                triple(bank[7][:, :], lambda a, p: ctxT[:, k % 2, a, :], lambda m, p: woutT[:, m, k, :], [0]).then_inc(S["w2_mm"], 1)
            gamma(8)
            pe.wait_ge(S["w2_lo"], K)

            def turn_w(i, g):
                pe.wait_ge(S["wr_q"], i + 1)
                n = 3 * i + g
                if n >= 2:
                    pe.wait_ge(S["wr_lo"], n - 1)
                for k in range(K):
                    ins = pe.transpose(bank[6 + n % 2][:, k * 128:(k + 1) * 128], wa[:, i % 2, 4 * g + k, :], ident[:])
                ins.then_inc(S["wr_T"], 1)

            for t in range(NT):
                mix(t)
                if t == 0:
                    gamma(9)
                if t >= 3:
                    turn_x1(t - 3)
                if t >= 7:
                    turn_w(0, t - 7)
            for t in range(NT - 3, NT - 1):
                turn_x1(t)

            u = 0
            for i in range(FT):
                pe.wait_ge(S["wr_lo"], 3 * i + 2)
                for c, (n0, nn) in enumerate(NC3):
                    if i == 0:
                        pe.wait_ge(S["x2_lo"], TILES_OF[c])
                    if u >= 3:
                        pe.wait_ge(S["hf_d"], u - 2)
                    for z in range(2):
                        ins = triple(bank[2 * c + z][:, 0:nn], lambda a, k: wgu[:, i % 2, a, (z * K + k) * 128:(z * K + k + 1) * 128],
                                     lambda m, k: qT[:, m, k, n0:n0 + nn], range(K))
                    ins.then_inc(S["gu_mm"], 1)
                    u += 1
                    if i == 0 and c == 0:
                        turn_x1(NT - 1)
                    if i + 1 < FT:
                        turn_w(i + 1, c)
            pe.wait_ge(S["wr_lo"], 3 * FT)
            for t in range(NT):
                need = max(c for c, (n0, nn) in enumerate(NC3) if n0 < (t + 1) * P) + 1
                pe.wait_ge(S["h_lo"], 3 * (FT - 1) + need)
                pe.wait_ge(S["h_hi"], 3 * (FT - 1) + need)
                if t >= 2:
                    pe.wait_ge(S["dn_d"], t - 1)
                triple(bank[t % 2][0:P, :], lambda a, i: hT[:, a, i, t * P:(t + 1) * P], lambda m, i: wdT[:, m, i, :], range(FT)).then_inc(S["dn_mm"], 1)

        @block.scalar
        def _(s):
            def prep_out(n):
                g, k = n // K, n % K
                s.wait_ge(S["prep_T"], n + 1)
                if n >= 2:
                    s.wait_ge(S["prep_lo"], n - 1)
                by = gcol[:, k:k + 1] if g < 3 else W_SCALE
                to = wqkvT[:, 0, k, g * D:(g + 1) * D] if g < 3 else woutT[:, 0, k, :]
                s.activation(to, bank[6 + n % 2][:, :], ACT.Copy, scale=by)
                s.activation(stage_w[:, n % 2, :], bank[6 + n % 2][:, :], ACT.Copy, scale=by).then_inc(S["prep_out"], 1)

            def counts_out(b):
                s.wait_ge(S["cnt_mm"], b + 1)
                if b:
                    s.wait_ge(S["cnt_lo"], b)
                for c, (n0, nn) in enumerate(NC3):
                    p = bank[3 * (b % 2) + c][0:P, 0:nn]
                    s.activation(counts[:, b, n0:n0 + nn], p, ACT.Copy, accum_out=indeg[:, 3 * b + c:3 * b + c + 1])
                    s.activation(stage_c[:, n0:n0 + nn], p, ACT.Copy).then_inc(S["cnt_out"], 1)

            def xT_high(t):
                s.wait_ge(S["xT_done"], t + 1)
                if t >= 2:
                    s.wait_ge(S["alpha_mm"], t - 1)
                s.activation(xT[:, t % 2, 0, :, :], tiles(bank[6 if t == 0 else 5]), ACT.Copy, scale=X_SCALE).then_inc(S["xT_hi"], 1)

            s.wait_ge(S["gcol_d"], 1)
            for b in range(NT):
                if b < 2 * K:
                    prep_out(2 * b)
                    prep_out(2 * b + 1)
                if b >= 8:
                    i = b - 8
                    s.wait_ge(S[f"raw_in{i}"], 48)
                    s.activation(wcn[:, 0, :, i * D:(i + 1) * D], raw[:, i, :, :], ACT.Copy, scale=W_SCALE).then_inc(S["wcn_own"], 1)
                    s.wait_ge(S["wcn_own"], i + 1)
                    s.activation(raw[:, i, :, :], raw[:, i, :, :], ACT.Copy, scale=W_SCALE).then_inc(S["wcn_hi"], 1)
                if b == NT - 1:
                    xT_high(0)
                counts_out(b)
            for t in range(NT):
                s.wait_ge(S["k_mm"], t + 1)
                if t == 0:
                    s.wait_ge(S["wcn_lo"], 2)
                s.activation(kf[:, t, :], bank[1][0:P, :], ACT.Copy, scale=r2k[:, t:t + 1]).then_inc(S["k_out"], 1)
                s.wait_ge(S["q_sub"], t + 1)
                s.activation(qe, qe, ACT.Exp, scale=r2k[:, t:t + 1]).then_inc(S["q_exp"], 1)
                s.wait_ge(S["v_mm"], t + 1)
                if t == 0:
                    s.wait_ge(S["v_one"], 2)
                s.activation(vp[:, 0, t, :, 0:128], bank[2][0:P, :].rearrange("p (k e) -> p k e", k=K), ACT.Copy, scale=r2v[:, t:t + 1]).then_inc(S["v_hi"], 1)
                if t + 1 < NT:
                    xT_high(t + 1)
                s.wait_ge(S["beta_mm"], t + 1)
                s.activation(betas[:, 0, t, :], bank[0][0:P, :], ACT.Copy, scale=1.0 / W_SCALE).then_inc(S["beta_hi"], 1)
                s.wait_ge(S["qT_mm"], t + 1)
                s.activation(qT[:, 0, :, t * P:(t + 1) * P], tiles(bank[6]), ACT.Copy, scale=Q_SCALE).then_inc(S["qT_hi"], 1)
            for t in range(NT):
                s.wait_ge(S["k_sub"], t + 1)
                if t >= 2:
                    s.wait_ge(S["ek_lo"], t - 1)
                s.activation(ering[:, t % 2, :], kf[:, t, :], ACT.Exp).then_inc(S["k_exp"], 1)
                s.wait_ge(S["k_exp"], t + 1)
                s.activation(ek[:, t, 0, :], ering[:, t % 2, :], ACT.Copy).then_inc(S["ek_hi"], 1)
            s.wait_ge(S["ctx_zero"], 1)
            for k in range(K):
                s.wait_ge(S["ctxT_mm"], k + 1)
                if k >= 2:
                    s.wait_ge(S["w2_mm"], k - 1)
                for h in range(2):
                    d = slice(64 * h, 64 * h + 64)
                    ins = s.activation(ctxT[d, k % 2, 0, d], bank[6][d, d], ACT.Copy, scale=C_SCALE)
                ins.then_inc(S["ctx_hi"], 1)
                s.wait_ge(S["w2_mm"], k + 1)
                s.activation(w2[:, 0, k, :], bank[7][:, :], ACT.Copy, scale=1.0 / W_SCALE).then_inc(S["w2_hi"], 1)

            def mix_out(t):
                m = mst[:, t % 2, :]
                s.wait_ge(S["mst_p"], t + 1)
                if t >= 2:
                    s.wait_ge(S["x1_d"], t - 1)
                s.activation(xn[:, t % 2, :], bank[2 + t % 2][0:P, :], ACT.Identity, bias=m[:, 5:6], scale=m[:, 4:5]).then_inc(S["mix_n"], 1)

            def x2_high(t):
                s.wait_ge(S["x2T_mm"], t + 1)
                s.activation(qT[:, 0, :, t * P:(t + 1) * P], tiles(bank[4 + t % 2]), ACT.Copy, scale=X_SCALE).then_inc(S["x2_hi"], 1)

            def w_high(i, g):
                n = 3 * i + g
                s.wait_ge(S["wr_T"], n + 1)
                if g < 2 and i >= 2:
                    s.wait_ge(S["gu_mm"], 3 * (i - 1))
                to = wgu[:, i % 2, 0, g * D:(g + 1) * D] if g < 2 else wdT[:, 0, i, :]
                s.activation(to, bank[6 + n % 2][:, :], ACT.Copy, scale=W_SCALE).then_inc(S["wr_hi"], 1)

            for t in range(NT):
                mix_out(t)
                if t >= 3:
                    x2_high(t - 3)
                if t >= 7:
                    w_high(0, t - 7)
            for t in range(NT - 3, NT - 1):
                x2_high(t)
            u = 0
            for i in range(FT):
                for c, (n0, nn) in enumerate(NC3):
                    if i == 0 and c == 1:
                        x2_high(NT - 1)
                    s.wait_ge(S["gu_mm"], u + 1)
                    if u >= 2:
                        s.wait_ge(S["hf_d"], u - 1)
                    s.activation(sg[:, u % 2, 0:nn], bank[2 * c][:, 0:nn], ACT.Silu, scale=UNDO).then_inc(S["sg_d"], 1)
                    s.wait_ge(S["hf_d"], u + 1)
                    s.activation(hT[:, 0, i, n0:n0 + nn], hf[:, u % 2, 0:nn], ACT.Copy).then_inc(S["h_hi"], 1)
                    u += 1
                    if i + 1 < FT:
                        w_high(i + 1, c)

        @block.vector
        def _(v):
            n_own = [0]

            def own(ins):
                n_own[0] += 1
                ins.then_inc(S["v_own"], 1)
                v.wait_ge(S["v_own"], n_own[0])

            def qT_low(t):
                v.wait_ge(S["qT_hi"], t + 1)
                d = slice(t * P, (t + 1) * P)
                v.scalar_tensor_tensor(qT[:, 1, :, d], tiles(bank[6]), Q_SCALE, qT[:, 0, :, d], ALU.mult, ALU.subtract).then_inc(S["qT_lo"], 1)

            v.wait_ge(S["edge_in"], 32)
            v.tensor_copy(edges.rearrange("r a h e -> r a (h e)"), edges_i).then_inc(S["edge_f"], 1)
            v.wait_ge(S["edge_f"], 1)
            own(v.tensor_reduce(ext[:, 0, :], edges[:, 1, :, :], AX.X, ALU.max))
            own(v.tensor_reduce(ext[:, 1, :], edges[:, 1, :, :], AX.X, ALU.min))
            own(v.tensor_scalar(ext[:, 1, :], ext[:, 1, :], float(P - 1), None, ALU.subtract))
            v.wait_ge(S["g_const"], 7)
            for h in range(2):
                own(v.tensor_scalar(ov[:, h, 0, :], block_at[:], ext[:, 0, h:h + 1], None, ALU.is_le))
                own(v.tensor_scalar(ov[:, h, 1, :], block_at[:], ext[:, 1, h:h + 1], None, ALU.is_ge))
                own(v.tensor_tensor(ov[:, h, 0, :], ov[:, h, 0, :], ov[:, h, 1, :], ALU.mult))
                v.tensor_scalar(ov[:, h, 2, :], ov[:, h, 0, :], chunk_up[:, h:h + 1], None, ALU.mult)
                ins = v.tensor_scalar(ov[:, h, 3, :], ov[:, h, 0, :], chunk_dn[:, h:h + 1], None, ALU.mult)
            ins.then_inc(S["bound_v"], 1)
            v.wait_ge(S["bT_mm"], 1)
            for h in range(2):
                for a in range(2):
                    v.tensor_copy(eT[:, h:NCH:2, a], bank[7 - h][0:P, a * ROWS:(a + 1) * ROWS])
            v.wait_ge(S["bT_mm"], 2)
            own(v.tensor_reduce(bounds[:, 0:2], bank[0][0:NT, 0:4 * ROWS].rearrange("p (a j) -> p a j", a=2), AX.X, ALU.max))
            own(v.tensor_scalar(bounds[:, 1:2], bounds[:, 1:2], -1.0, float(NCH), ALU.mult, ALU.add))
            own(v.tensor_scalar(bounds[:, 2:3], bounds[:, 1:2], float(LEAST), None, ALU.add))
            v.tensor_tensor(bounds[:, 0:1], bounds[:, 0:1], bounds[:, 2:3], ALU.max).then_inc(S["bound_v"], 1)
            v.wait_ge(S["bp_mm"], 1)
            v.tensor_copy(brow[:], bank[1][0:1, 0:2 * NT]).then_inc(S["brow_d"], 1)
            v.wait_ge(S["gT_mm"], 1)
            v.tensor_scalar(gcol[:], bank[2][:, 0:K], W_SCALE, None, ALU.mult).then_inc(S["gcol_d"], 1)
            own(v.tensor_scalar(iota_b[:], iota_n[:, 0:P], float(P), None, ALU.subtract))
            v.wait_ge(S["brow_d"], 1)
            visit = v.alloc_register("dve_visit")
            v.reg_mov(visit, 0)

            def stats(t):
                v.wait_ge(S[f"x_in{t // 2}"], 16)
                own(v.bn_stats(st6[:, t, :], xr[:, t, :]))
                v.bn_aggr(mv[:, t, :], st6[:, t, :]).then_inc(S["stats_v"], 1)

            def norm(t):
                if t >= 2:
                    v.wait_ge(S["xT_done"], t - 1)
                v.tensor_scalar(xn[:, t % 2, :], xr[:, t, :], mv[:, t, 0:1], rstd[:, t:t + 1], ALU.subtract, ALU.mult).then_inc(S["xn_ready"], 1)

            def xT_low(t):
                v.wait_ge(S["xT_hi"], t + 1)
                v.scalar_tensor_tensor(xT[:, t % 2, 1, :, :], tiles(bank[6 if t == 0 else 5]), X_SCALE, xT[:, t % 2, 0, :, :], ALU.mult, ALU.subtract).then_inc(S["xT_lo"], 1)

            for b in range(NT):
                v.tensor_scalar(iota_b[:], iota_b[:], float(P), None, ALU.add).then_inc(S["iota_d"], 1)
                v.wait_ge(S["iota_d"], b + 1)
                hi = v.value_load(brow[0:1, b:b + 1], min_val=LEAST, max_val=NCH + LEAST)
                lo = v.value_load(brow[0:1, b + NT:b + NT + 1], min_val=0, max_val=NCH)
                with v.Fori(lo, hi, GRP) as j:
                    w = v.snap(visit, min_val=0, max_val=NT * (NCH + 3 * GRP))
                    for q in range(GRP):
                        if q % 2 == 0:
                            v.wait_ge(S["oh_used"], w + (q + 2))
                        at = eT[:, bass.ds(j + q, 1), :].rearrange("p a e -> p (a e)")
                        v.tensor_scalar(oh_src[:, q, :], iota_n[:], at[:, 0:1], None, ALU.is_equal)
                        v.tensor_scalar(oh_dst[:, q, 0:P], iota_b[:], at[:, 1:2], None, ALU.is_equal).then_inc(S["oh_ready"], 1)
                    v.reg_add(visit, visit, GRP)
                if 1 <= b <= NT // 2:
                    stats(2 * b - 2)
                    stats(2 * b - 1)
                if b == NT - 2:
                    v.wait_ge(S["r_ready"], 1)
                    norm(0)
                    norm(1)
            xT_low(0)
            v.wait_ge(S["cnt_out"], 3 * NT)
            v.tensor_reduce(indeg[:, 3 * NT:3 * NT + 1], indeg[:, 0:3 * NT], AX.X, ALU.max).then_inc(S["flag_c"], 1)

            heads = lambda ap: ap.rearrange("p (h d) -> p h d", d=HEAD)
            spread = lambda ap: ap.rearrange("p (h o) -> p h o", o=1).broadcast_to([P, HEADS, HEAD])
            for t in range(NT):
                v.wait_ge(S["k_out"], t + 1)
                if t == 0:
                    v.tensor_copy(kmax, kf[:, 0, :]).then_inc(S["kmax_d"], 1)
                else:
                    v.wait_ge(S["kmax_d"], t)
                    v.tensor_tensor(kmax, kmax, kf[:, t, :], ALU.max).then_inc(S["kmax_d"], 1)
                v.wait_ge(S["q_mm"], t + 1)
                v.tensor_reduce(qmx[:], heads(bank[3][0:P, :]), AX.X, ALU.max).then_inc(S["q_max"], 1)
                v.wait_ge(S["q_max"], t + 1)
                if t:
                    v.wait_ge(S["q_norm"], t)
                v.tensor_tensor(heads(qe), heads(bank[3][0:P, :]), spread(qmx[:]), ALU.subtract).then_inc(S["q_sub"], 1)
                v.wait_ge(S["v_hi"], t + 1)
                v.scalar_tensor_tensor(vp[:, 1, t, :, 0:128], bank[2][0:P, :].rearrange("p (k e) -> p k e", k=K), r2v[:, t:t + 1], vp[:, 0, t, :, 0:128], ALU.mult, ALU.subtract).then_inc(S["v_lo"], 1)
                v.wait_ge(S["q_exp"], t + 1)
                v.tensor_reduce(qsum[:], heads(qe), AX.X, ALU.add).then_inc(S["q_sum"], 1)
                v.wait_ge(S["q_sum"], t + 1)
                v.reciprocal(qsum[:], qsum[:]).then_inc(S["q_rec"], 1)
                v.wait_ge(S["q_rec"], t + 1)
                if t:
                    v.wait_ge(S["qT_mm"], t)
                v.tensor_tensor(heads(qn), heads(qe), spread(qsum[:]), ALU.mult).then_inc(S["q_norm"], 1)
                if t + 2 < NT:
                    norm(t + 2)
                if t + 1 < NT:
                    xT_low(t + 1)
                if t == 2:
                    v.wait_ge(S["flag_mm"], 1)
                    own(v.tensor_reduce(flag_f[:], bank[7][0:1, 0:P], AX.X, ALU.max))
                    v.tensor_scalar(flag[:], flag_f[:], 2048.0, None, ALU.is_gt).then_inc(S["flag_d"], 1)
                if t == 4:
                    v.wait_ge(S["cn_mm"], 1)
                    own(v.reciprocal(crec[:], bank[7][0:P, 0:NT]))
                    v.tensor_scalar(crec[:], crec[:], 1.0 / X_SCALE, None, ALU.mult).then_inc(S["crec_d"], 1)
                v.wait_ge(S["beta_hi"], t + 1)
                v.scalar_tensor_tensor(betas[:, 1, t, :], bank[0][0:P, :], 1.0 / W_SCALE, betas[:, 0, t, :], ALU.mult, ALU.subtract).then_inc(S["beta_lo"], 1)
                if t == NT - 1:
                    v.wait_ge(S["kmT_mm"], 1)
                    v.tensor_reduce(kmaxc[:], tiles(bank[7]), AX.X, ALU.max).then_inc(S["kmc_d"], 1)
                v.wait_ge(S["alpha_mm"], t + 1)
                v.wait_ge(S["xb_done"], t + 1)
                v.scalar_tensor_tensor(xr[:, t, :], bank[4][0:P, :], UNDO, xr[:, t, :], ALU.mult, ALU.add).then_inc(S["acc_done"], 1)
                if t < NT - 1:
                    qT_low(t)

            def gamma_out(t):
                v.wait_ge(S["gam_mm"], t + 1)
                v.wait_ge(S["acc_done"], t + 1)
                if t == 0:
                    v.wait_ge(S["crec_d"], 1)
                v.scalar_tensor_tensor(xr[:, t, :], bank[t % 2][0:P, :], crec[:, t:t + 1], xr[:, t, :], ALU.mult, ALU.add).then_inc(S["gam_d"], 1)

            v.wait_ge(S["kmb_mm"], 1)
            for t in range(NT):
                v.tensor_tensor(kf[:, t, :], kf[:, t, :], bank[7][0:P, :], ALU.subtract).then_inc(S["k_sub"], 1)
                if t == 2:
                    qT_low(NT - 1)
            for t in range(4):
                gamma_out(t)
            v.wait_ge(S["ctx_mm"], 1)
            v.wait_ge(S["ctx_zero"], 1)

            def ctx_norm(k):
                own(v.reciprocal(krec[:, k:k + 1], bank[2 + k][:, 128:129]))
                if k >= 2:
                    v.wait_ge(S["ctxT_mm"], k - 1)
                v.tensor_scalar(ctxn[:, k % 2, :], bank[2 + k][:, 0:128], krec[:, k:k + 1], 1.0 / X_SCALE, ALU.mult, ALU.mult).then_inc(S["ctx_n"], 1)

            ctx_norm(0)
            for k in range(K):
                v.wait_ge(S["ctx_hi"], k + 1)
                for h in range(2):
                    d = slice(64 * h, 64 * h + 64)
                    ins = v.scalar_tensor_tensor(ctxT[d, k % 2, 1, d], bank[6][d, d], C_SCALE, ctxT[d, k % 2, 0, d], ALU.mult, ALU.subtract)
                ins.then_inc(S["ctx_lo"], 1)
                if k + 1 < K:
                    ctx_norm(k + 1)
                gamma_out(4 + k)
                v.wait_ge(S["w2_hi"], k + 1)
                v.scalar_tensor_tensor(w2[:, 1, k, :], bank[7][:, :], 1.0 / W_SCALE, w2[:, 0, k, :], ALU.mult, ALU.subtract).then_inc(S["w2_lo"], 1)
            gamma_out(8)

            def mix_stats(t):
                v.wait_ge(S["mix_mm"], t + 1)
                if t >= 2:
                    v.wait_ge(S["mst_p"], t - 1)
                own(v.bn_stats(st6[:, t, :], bank[2 + t % 2][0:P, :]))
                v.bn_aggr(mst[:, t % 2, 0:2], st6[:, t, :]).then_inc(S["mst_v"], 1)

            def x1_sum(t):
                v.wait_ge(S["mix_g"], t + 1)
                v.wait_ge(S["gam_d"], t + 1)
                v.tensor_tensor(xr[:, t, :], xr[:, t, :], xn[:, t % 2, :], ALU.add).then_inc(S["x1_d"], 1)
                v.wait_ge(S["x1_d"], t + 1)
                own(v.bn_stats(st6x[:, t, :], xr[:, t, :]))
                v.bn_aggr(xst[:, t % 2, 0:2], st6x[:, t, :]).then_inc(S["x1_st"], 1)

            def x1_norm(t):
                v.wait_ge(S["x1_p"], t + 1)
                if t >= 2:
                    v.wait_ge(S["x2T_mm"], t - 1)
                v.tensor_scalar(xn2[:, t % 2, :], xr[:, t, :], xst[:, t % 2, 0:1], xst[:, t % 2, 3:4], ALU.subtract, ALU.mult).then_inc(S["x2_n"], 1)

            def x2_low(t):
                v.wait_ge(S["x2_hi"], t + 1)
                d = slice(t * P, (t + 1) * P)
                v.scalar_tensor_tensor(qT[:, 1, :, d], tiles(bank[4 + t % 2]), X_SCALE, qT[:, 0, :, d], ALU.mult, ALU.subtract).then_inc(S["x2_lo"], 1)

            def quantise(i):
                v.wait_ge(S[f"wr_in{i % 2}"], 48 * (i // 2 + 1))
                v.tensor_reduce(gsum[:], wraw[:, i % 2, :, :], AX.X, ALU.add, apply_absolute_value=True).then_inc(S["wr_abs"], 1)
                v.wait_ge(S["wr_abs"], i + 1)
                if i:
                    v.wait_ge(S["wr_b"], i)
                own(v.tensor_scalar(gthr[:, 0, :], gsum[:], 1.0 / 128, EPS, ALU.mult, ALU.add))
                own(v.tensor_scalar(gthr[:, 1, :], gthr[:, 0, :], 0.5, None, ALU.mult))
                v.tensor_scalar(gthr[:, 2, :], gthr[:, 0, :], -0.5, None, ALU.mult).then_inc(S["wr_thr"], 1)
                if i >= 2:
                    v.wait_ge(S["wr_T"], 3 * (i - 1))
                for j in range(12):
                    ins = v.tensor_scalar(wa[:, i % 2, j, :], wraw[:, i % 2, j, :], gthr[:, 1, j:j + 1], gthr[:, 0, j:j + 1], ALU.is_gt, ALU.mult)
                ins.then_inc(S["wr_a"], 1)

            def w_low(i, g):
                n = 3 * i + g
                v.wait_ge(S["wr_hi"], n + 1)
                d = slice(g * D, (g + 1) * D)
                hi, lo = [(wgu[:, i % 2, a, d] if g < 2 else wdT[:, a, i, :]) for a in range(2)]
                v.scalar_tensor_tensor(lo, bank[6 + n % 2][:, :], W_SCALE, hi, ALU.mult, ALU.subtract).then_inc(S["wr_lo"], 1)

            for t in range(NT + 2):
                if t < NT:
                    mix_stats(t)
                if t == 0:
                    gamma_out(9)
                if 1 <= t <= NT:
                    x1_sum(t - 1)
                if t >= 2:
                    x1_norm(t - 2)
                if 4 <= t:
                    x2_low(t - 4)
                if t == 3:
                    quantise(0)
                if t == 6:
                    quantise(1)
                if 8 <= t < NT:
                    w_low(0, t - 8)
            w_low(0, 2)
            x2_low(NT - 2)

            u = 0
            for i in range(FT):
                if i + 2 < FT:
                    quantise(i + 2)
                for c, (n0, nn) in enumerate(NC3):
                    if i == 0 and c == 1:
                        x2_low(NT - 1)
                    v.wait_ge(S["sg_d"], u + 1)
                    if u >= 2:
                        v.wait_ge(S["h_hi"], u - 1)
                    v.scalar_tensor_tensor(hf[:, u % 2, 0:nn], bank[2 * c + 1][:, 0:nn], H_SCALE * UNDO, sg[:, u % 2, 0:nn], ALU.mult, ALU.mult).then_inc(S["hf_d"], 1)
                    v.wait_ge(S["h_hi"], u + 1)
                    v.tensor_tensor(hT[:, 1, i, n0:n0 + nn], hf[:, u % 2, 0:nn], hT[:, 0, i, n0:n0 + nn], ALU.subtract).then_inc(S["h_lo"], 1)
                    u += 1
                    if i + 1 < FT:
                        w_low(i + 1, c)
            for t in range(NT):
                v.wait_ge(S["dn_mm"], t + 1)
                v.scalar_tensor_tensor(xr[:, t, :], bank[t % 2][0:P, :], 1.0 / (W_SCALE * H_SCALE), xr[:, t, :], ALU.mult, ALU.add).then_inc(S["dn_d"], 1)



_INS = ["x", "src", "dst", "L0_gnn_wc", "L0_gnn_wn", "L0_gnn_bias", "L0_mix_norm_gamma", "L0_mix_w_qkv", "L0_mix_w_out",
        "L0_mix_out_gamma", "L0_ffn_w_gate", "L0_ffn_w_up", "L0_ffn_w_down"]


def kernel(**inputs):
    import numpy as np
    import concourse.bacc as bacc
    import concourse.bass_utils as bass_utils

    nc = bacc.Bacc("TRN2", target_bir_lowering=False, num_devices=1)
    arrays, args = {}, []
    for name in _INS:
        a = np.ascontiguousarray(inputs[name])
        arrays[f"in_{name}"] = a
        args.append(nc.dram_tensor(f"in_{name}", a.shape, mybir.dt.from_np(a.dtype), kind="ExternalInput").ap())
    out = nc.dram_tensor("out", inputs["x"].shape, F32, kind="ExternalOutput").ap()
    gps_layer(nc, *args, out)
    return bass_utils.run_bass_kernel_spmd(nc, [arrays], core_ids=[0]).results[0]["out"]
```

```python
from contextlib import ExitStack

import concourse.bass as bass
from concourse import mybir

F32 = mybir.dt.float32
F16 = mybir.dt.float16
I32 = mybir.dt.int32
F8 = mybir.dt.float8e4
ALU = mybir.AluOpType
ACT = mybir.ActivationFunctionType
AX = mybir.AxisListType

EPS = 1e-5
W_SCALE = 64.0
X_SCALE = 32.0
Q_SCALE = 64.0
C_SCALE = 256.0
H_SCALE = 16.0
HEAD = 64
PARTS = ((0, 0), (1, 0), (0, 1))


def gps_layer(nc, x, src, dst, wc, wn, bias, g_norm, w_qkv, w_out, g_out, w_gate, w_up, w_down, out):
    N, D = x.shape
    E, = src.shape
    F = w_gate.shape[0]
    P = 125
    NT = N // P
    NCH = E // P
    ROWS = NCH // 2
    SPAN = 50
    NB = N // SPAN
    PAIR = 2 * P // SPAN
    PIECES = 6
    AT_PREP = 5
    POOL_GROUPS = 10
    AHEAD = 5
    MOST = 8
    GRP = 4
    K = D // 128
    FT = F // 128
    HEADS = D // HEAD
    NC3 = [(0, 417), (417, 417), (834, 416)]
    TILES_OF = [-(-(a + n) // P) for a, n in NC3]
    MIX = 1.0 / (Q_SCALE * C_SCALE * HEAD ** 0.5)
    UNDO = 1.0 / (W_SCALE * X_SCALE)
    assert N == NT * P and E == 2 * ROWS * P and D == 512 and w_qkv.shape[0] == 3 * D and F == FT * 128
    assert ROWS <= 128 and SPAN * NT <= 512 and 2 * P % SPAN == 0

    with ExitStack() as ctx:
        def sb(name, shape, dt):
            return ctx.enter_context(nc.sbuf_tensor(name, shape, dt))

        def sem(name):
            return ctx.enter_context(nc.semaphore(name))

        bank = [ctx.enter_context(nc.psum_tensor(f"bank{i}", [128, 512], F32)) for i in range(8)]

        ident = sb("ident", [128, 128], F32)
        ident_h = sb("ident_h", [128, 128], F16)
        iota_key = sb("iota_key", [P, NT * SPAN], F16)
        iota_lane = sb("iota_lane", [P, 128], F16)
        block_at = sb("block_at", [ROWS, NB], F32)
        chunk_up = sb("chunk_up", [ROWS, 2], F32)
        chunk_dn = sb("chunk_dn", [ROWS, 2], F32)
        ones_h = sb("ones_h", [P, 1], F16)
        halfpow = sb("halfpow", [P, NT], F32)
        rows_b = sb("rows_b", [P, D], F32)
        grow = sb("grow", [K, 128], F32)
        gcol = sb("gcol", [128, K], F32)
        st6 = sb("st6", [P, NT, 6], F32)
        st6x = sb("st6x", [P, NT, 6], F32)
        mv = sb("mv", [P, NT, 2], F32)
        rstd = sb("rstd", [P, NT], F32)
        nmean = sb("nmean", [P, NT], F32)
        nvar = sb("nvar", [P, NT], F32)
        r2k = sb("r2k", [P, NT], F32)
        r2v = sb("r2v", [P, NT], F32)
        qmx = sb("qmx", [P, HEADS], F32)
        qsum = sb("qsum", [P, HEADS], F32)
        kmaxc = sb("kmaxc", [128, K], F32)
        krec = sb("krec", [128, K], F32)
        crec = sb("crec", [P, NT], F32)
        span = sb("span", [1, 1], F32)
        mst = sb("mst", [P, 2, 6], F32)
        xst = sb("xst", [P, 2, 5], F32)
        ext = sb("ext", [ROWS, 2, 2], F32)
        bounds = sb("bounds", [NB, 3], F32)
        brow = sb("brow", [1, 2 * NB + 1], I32)
        gsum = sb("gsum", [128, 2, 12], F32)
        gthr = sb("gthr", [128, 2, 3, 12], F32)
        xr = sb("xr", [P, NT, D], F32)
        betas = sb("betas", [P, 2, NT, D], F16)
        qT = sb("qT", [128, 2, K, NT * P], F16)
        xn = sb("xn", [P, 2, D], F32)
        oh_lane1 = sb("oh_lane1", [P, MOST, 126], F16)
        small = sb("small", [128, 2694], F32)
        zone = sb("zone", [128, 31984], F32)

        def view(at, shape, dt, zone=zone):
            n = 1
            for s in shape[1:]:
                n *= s
            words = {F32: n, I32: n, F16: n // 2, F8: n // 4}[dt]
            v = zone[0:shape[0], at:at + words]
            if dt != F32:
                v = v.bitcast(dt)
            names = "abcd"[:len(shape) - 1]
            if len(shape) > 2:
                v = v.rearrange(f"p ({' '.join(names)}) -> p {' '.join(names)}", **{c: s for c, s in zip(names, shape[1:])})
            return v

        AT_OUT, AT_CN, AT_QKV, AT_KV = 9376, 11424, 15520, 21664
        counts = view(0, [P, NT, N], F16)
        counts_lo = view(6250, [P, NT, N], F8)
        woutT = view(AT_OUT, [128, 2, K, D], F16)
        wcn = view(AT_CN, [128, 2, K, 2 * D], F16)
        wqkvT = view(AT_QKV, [128, 2, K, 3 * D], F16)
        kf = view(AT_KV, [P, NT, D], F32)
        ek = view(AT_KV, [P, NT, 2, D], F16)
        vp = view(AT_KV + 5120, [P, 2, NT, K, 130], F16)
        raw = view(AT_KV, [128, 2, K, D], F32)
        stage_w = view(AT_KV + 4096, [128, 2, D], F32)
        oh_key = view(AT_KV + 5120, [P, 2 * MOST, NT * SPAN], F16)
        oh_lane = [view(2054, [P, MOST, 126], F16, small), oh_lane1]
        stage_c = view(AT_KV + 9120, [P, NT * SPAN], F32)
        stage_t = view(AT_KV + 9620, [P, 4 * P], F32)
        e_lane = view(AT_KV + 10120, [P, NCH + MOST], F32)
        e_key = view(1876, [P, NCH + MOST], F32, small)
        cs_hi = [view(0, [P, NT, 2 * P], F16, small), view(AT_OUT, [P, NT, 2 * P], F16)]
        cs_lo = [view(1250, [P, NT, 2 * P], F8, small), view(AT_OUT + 1250, [P, NT, 2 * P], F8)]
        edges_i = view(0, [ROWS, 2, 2 * P], I32, small)
        edges = view(500, [ROWS, 2, 2, P], F32, small)
        ov = view(1000, [ROWS, 2, 4, NB], F32, small)
        tile_of = view(1200, [ROWS, 2, 2 * P], F32, small)
        qe, qn = xn[:, 0, :], xn[:, 1, :]
        ering = view(0, [P, 2, D], F32, small)
        kmax = view(2040, [P, D], F32, small)
        w2 = view(AT_CN, [128, 2, K, D], F16)
        ctxn = view(AT_CN + 2048, [128, 2, 128], F32)
        ctxT = view(AT_CN + 2304, [128, 2, 2, 128], F16)
        xn2 = view(0, [P, 2, D], F32, small)
        sg = view(1024, [128, 2, 417], F32, small)
        hf = view(1860, [128, 2, 417], F32, small)
        wraw = view(AT_QKV, [128, 2, 12, 128], F32)
        wa = view(AT_QKV + 3072, [128, 2, 12, 128], F32)
        wb_first = view(1024, [128, 12, 128], F32, small)
        wb = [view(at, [128, 12, 128], F32) for at in (AT_KV, FT * N)]
        wgu = view(AT_KV + 1536, [128, 2, 2, 2 * K * 128], F16)
        wdT = view(AT_KV + 3584, [128, 2, FT, D], F16)
        hT = view(0, [128, 2, FT, N], F16)

        S = {}

        def sems(text):
            for n in text.split():
                S[n] = sem(n)

        sems("""v_own p_own edge_in small_in gain_in x_in0 x_in1 x_in2 x_in3 x_in4 raw_in0 raw_in1 wr_in0 wr_in1
            g_ident g_const stats_v gcol_d r_ready r2_ready gT_mm
            edge_f edge_k bound_v bT_mm bp_mm brow_d oh_ready ex_ready ex_used cnt_mm cs_out cs_lo t_mm t_out t_lo
            prep_T prep_out prep_lo wcn_own wcn_hi wcn_lo cn_mm crec_d
            xn_ready xT_done xT_hi xT_lo beta_mm k_mm v_mm q_mm alpha_mm
            beta_hi beta_lo k_out kmax_d v_hi v_lo q_max q_sub q_exp q_sum q_rec q_norm qT_mm qT_hi qT_lo
            xb_done acc_done kmT_mm kmc_d kmb_mm k_sub k_exp ek_hi ek_lo v_one ctx_mm ctx_n ctxT_mm
            ctx_zero ctx_hi ctx_lo w2_mm w2_hi w2_lo gam_mm gam_d mix_mm mst_v mst_p mix_n mix_g x1_d x1_st x1_p x2_n
            x2T_mm x2_hi x2_lo wr_abs wr_scale wr_thr wr_a wr_b wr_q wr_T wr_hi wr_lo gu_mm sg_d hf_d h_hi h_lo dn_mm dn_d
            out_0 out_1""")

        def tiles(b):
            return b[:, 0:K * P].rearrange("p (k n) -> p k n", k=K)

        block = ctx.enter_context(nc.Block())

        def hidden(buffer, part, i):
            return buffer[:, part, bass.ds(i, 1), :].rearrange("p o n -> p (o n)")

        def piece(n):
            u0 = n % 3 * 4
            return n // 3, slice(u0 * P, min(u0 + 4, NT) * P)

        def staged(n):
            return stage_c if n >= PIECES * (NB // PAIR - 1) and n % 2 else stage_t

        def bounds_at(engine, b):
            regs = [engine.alloc_register(f"bound_{b}_{n}") for n in range(2 * AHEAD)]
            engine.reg_load(regs, brow[0:1, 2 * b:2 * (b + AHEAD)])
            return {b + i: (engine.snap(regs[2 * i], min_val=0, max_val=NCH),
                            engine.snap(regs[2 * i + 1], min_val=0, max_val=NCH), regs[2 * i]) for i in range(AHEAD)}

        def pieces_at(b):
            pair, r = b // PAIR - 1, b % PAIR
            n = PIECES * pair
            return [] if pair < 0 else [n, n + 1] if r == 0 else [n + 1 + r]

        p0, w0 = PIECES * (NB // PAIR - 1), 3 * K
        TAIL = ([(0, w0), (0, w0 + 1)],
                [(1, p0), (1, p0 + 1), (0, w0 + 2), (1, p0 + 2), (1, p0 + 3)],
                [(0, w0 + 3), (1, p0 + 4), (1, p0 + 5)])

        def preps_at(b):
            n = b - AT_PREP
            return [n] if 0 <= n < 3 * K else []

        AT_TURN, AT_BIAS, AT_PRODUCT, AT_BETA = -1, 0, 1, 3

        def tile_at(b, first):
            return [t for t in range(NT) if t * 12 // 5 + first == b]

        @block.sync
        def _(sp):
            for a, e in enumerate((src, dst)):
                sp.dma_start(edges_i[:, a, :], e.rearrange("(r e) -> r e", e=2 * P)).then_inc(S["edge_in"], 16)
            sp.dma_start(grow[:], g_norm.rearrange("(k p) -> k p", p=128)).then_inc(S["small_in"], 16)
            sp.dma_start(rows_b[:], bias.rearrange("(a d) -> a d", a=1).broadcast_to([P, D])).then_inc(S["small_in"], 16)

            def load_raw(n):
                if n in (2, 3):
                    sp.wait_ge(S["wcn_lo"], n - 1)
                elif n >= 4:
                    sp.wait_ge(S["prep_T"], 4 * (n - 3))
                w = [wc, wn, w_qkv[0:D, :], w_qkv[D:2 * D, :], w_qkv[2 * D:3 * D, :], w_out][n]
                sp.dma_start(raw[:, n % 2, :, :], w.rearrange("(j p) c -> p j c", p=128)).then_inc(S[f"raw_in{n % 2}"], 16)

            for t in range(0, NT, 2):
                sp.dma_start(xr[:, t:t + 2, :], x[t * P:(t + 2) * P, :].rearrange("(t p) d -> p t d", p=P)).then_inc(S[f"x_in{t // 2}"], 16)
                if t < 4:
                    load_raw(t // 2)
            for n in range(2, 6):
                load_raw(n)
            sp.wait_ge(S["xb_done"], NT)
            sp.dma_start(rows_b[:], g_out.rearrange("(a d) -> a d", a=1).broadcast_to([P, D])).then_inc(S["gain_in"], 16)
            sp.wait_ge(S["v_mm"], NT)
            for i in range(FT):
                if i >= 2:
                    sp.wait_ge(S["wr_a"], i - 1)
                    sp.wait_ge(S["wr_b"], i - 1)
                f = slice(i * 128, (i + 1) * 128)
                into = wraw[:, i % 2, :, :]
                done = S[f"wr_in{i % 2}"]
                sp.dma_start(into[:, 0:4, :], w_gate[f, :].rearrange("p (k d) -> p k d", d=128)).then_inc(done, 16)
                sp.dma_start(into[:, 4:8, :], w_up[f, :].rearrange("p (k d) -> p k d", d=128)).then_inc(done, 16)
                sp.dma_start(into[:, 8:12, :], w_down[:, f].rearrange("(k p) d -> p k d", p=128)).then_inc(done, 16)
            for t in range(NT):
                sp.wait_ge(S["dn_d"], t + 1)
                sp.dma_start(out[t * P:(t + 1) * P, :], xr[:, t, :]).then_inc(S[f"out_{t % 2}"], 16)
            for h in range(2):
                sp.wait_ge(S[f"out_{h}"], 16 * NT // 2)

        @block.gpsimd
        def _(g):
            n_own = [0]

            def own(ins):
                n_own[0] += 1
                ins.then_inc(S["p_own"], 1)
                g.wait_ge(S["p_own"], n_own[0])

            def iota(out, pattern, base, mult):
                g.iota(out, pattern, base=base, channel_multiplier=mult, allow_small_or_imprecise_dtypes=True).then_inc(S["g_const"], 1)

            iota(block_at[:], [[SPAN, NB]], 0, 0)
            iota(chunk_up[:], [[1, 2]], 1, 2)
            iota(chunk_dn[:], [[-1, 2]], NCH, -2)
            g.memset(ident[:], 0.0).then_inc(S["g_ident"], 1)
            g.wait_ge(S["g_ident"], 1)
            g.affine_select(out=ident[:], in_=ident[:], compare_op=ALU.not_equal, fill=1.0, base=0,
                            pattern=[[-1, 128]], channel_multiplier=1).then_inc(S["g_ident"], 1)
            iota(iota_key[:].rearrange("p (u d) -> p u d", u=NT), [[1, NT], [NT, SPAN]], 0, 0)
            iota(iota_lane[:], [[1, 128]], 0, 0)
            g.memset(e_lane[:, NCH:NCH + MOST], -1.0).then_inc(S["g_const"], 1)
            g.memset(e_key[:, NCH:NCH + MOST], -1.0).then_inc(S["g_const"], 1)
            g.memset(ones_h[:], 1.0).then_inc(S["g_const"], 1)
            g.memset(halfpow[:], -0.5).then_inc(S["g_const"], 1)
            g.wait_ge(S["g_ident"], 2)
            g.tensor_copy(ident_h[:], ident[:]).then_inc(S["g_const"], 1)
            g.wait_ge(S["g_const"], 10)

            def prep_low(n):
                g.wait_ge(S["prep_out"], n + 1)
                to, k = (wqkvT, n % K) if n < 3 * K else (woutT, n % K)
                d = slice((n // K) * D, (n // K + 1) * D) if n < 3 * K else slice(0, D)
                g.tensor_tensor(to[:, 1, k, d], stage_w[:, n % 2, :], to[:, 0, k, d], ALU.subtract).then_inc(S["prep_lo"], 1)

            def span_low(b):
                g.wait_ge(S["cs_out"], b + 1)
                pair, d = b // PAIR % 2, slice(b % PAIR * SPAN, (b % PAIR + 1) * SPAN)
                if b % PAIR == 0 and b >= 2 * PAIR:
                    g.wait_ge(S["t_mm"], PIECES * (b // PAIR - 1))
                g.tensor_tensor(cs_lo[pair][:, :, d], stage_c.rearrange("p (u d) -> p u d", u=NT), cs_hi[pair][:, :, d], ALU.subtract, saturate=False).then_inc(S["cs_lo"], 1)

            def piece_low(n):
                g.wait_ge(S["t_out"], n + 1)
                m, d = piece(n)
                g.tensor_tensor(counts_lo[:, m, d], staged(n)[:, 0:d.stop - d.start], counts[:, m, d], ALU.subtract, saturate=False).then_inc(S["t_lo"], 1)

            def x_scales(t0, t1):
                g.wait_ge(S["stats_v"], t1)
                c = slice(t0, t1)
                own(g.tensor_scalar(nvar[:, c], mv[:, c, 1], EPS, None, ALU.add))
                own(g.tensor_tensor(rstd[:, c], nvar[:, c], halfpow[:, c], ALU.pow))
                own(g.tensor_tensor(nmean[:, c], mv[:, c, 0], rstd[:, c], ALU.mult))
                g.tensor_scalar(nmean[:, c], nmean[:, c], -1.0, None, ALU.mult).then_inc(S["r_ready"], 1)
                own(g.tensor_tensor(nvar[:, c], rstd[:, c], rstd[:, c], ALU.mult))
                own(g.tensor_tensor(nvar[:, c], nvar[:, c], mv[:, c, 1], ALU.mult))
                own(g.tensor_scalar(nvar[:, c], nvar[:, c], EPS, None, ALU.add))
                own(g.tensor_tensor(r2k[:, c], nvar[:, c], halfpow[:, c], ALU.pow))
                own(g.tensor_scalar(r2v[:, c], r2k[:, c], X_SCALE * UNDO, None, ALU.mult))
                g.tensor_scalar(r2k[:, c], r2k[:, c], UNDO, None, ALU.mult).then_inc(S["r2_ready"], 1)

            def bias_in(t):
                g.wait_ge(S["xn_ready"], t + 1)
                g.tensor_tensor(xr[:, t, :], xr[:, t, :], rows_b[:], ALU.add).then_inc(S["xb_done"], 1)

            def wcn_low(i):
                g.wait_ge(S["wcn_hi"], i + 1)
                g.tensor_tensor(wcn[:, 1, :, i * D:(i + 1) * D], raw[:, i % 2, :, :], wcn[:, 0, :, i * D:(i + 1) * D], ALU.subtract).then_inc(S["wcn_lo"], 1)

            x_scales(0, 2)
            wcn_low(0)
            g.wait_ge(S["small_in"], 32)
            for b in range(NB):
                if b == 3:
                    x_scales(4, NT)
                if b == 0:
                    wcn_low(1)
                    x_scales(2, 4)
                span_low(b)
                for n in preps_at(b):
                    prep_low(n)
                for n in pieces_at(b):
                    piece_low(n)
                for t in tile_at(b, AT_BIAS):
                    bias_in(t)
            for at in TAIL[0] + TAIL[1] + TAIL[2]:
                (piece_low if at[0] else prep_low)(at[1])
            g.wait_ge(S["cnt_mm"], NB)
            g.wait_ge(S["t_lo"], 3 * NT)
            for h in range(2):
                g.memset(vp[:, h, :, :, 128:129].rearrange("p t k o -> p (t k) o"), 1.0 - h).then_inc(S["v_one"], 1)
            g.wait_ge(S["beta_mm"], NT)
            g.wait_ge(S["alpha_mm"], NT)
            g.memset(ctxT, 0.0).then_inc(S["ctx_zero"], 1)
            for t in range(NT):
                g.wait_ge(S["ek_hi"], t + 1)
                g.tensor_tensor(ek[:, t, 1, :], ering[:, t % 2, :], ek[:, t, 0, :], ALU.subtract).then_inc(S["ek_lo"], 1)
            def mix_stats(t):
                m = mst[:, t % 2, :]
                g.wait_ge(S["mst_v"], t + 1)
                if t >= 2:
                    g.wait_ge(S["mix_n"], t - 1)
                own(g.tensor_scalar(m[:, 2:3], m[:, 1:2], EPS / MIX ** 2, None, ALU.add))
                own(g.tensor_tensor(m[:, 4:5], m[:, 2:3], halfpow[:, 0:1], ALU.pow))
                g.tensor_scalar(m[:, 5:6], m[:, 0:1], m[:, 4:5], -1.0, ALU.mult, ALU.mult).then_inc(S["mst_p"], 1)

            def mix_gain(t):
                g.wait_ge(S["mix_n"], t + 1)
                g.tensor_tensor(xn[:, t % 2, :], xn[:, t % 2, :], rows_b[:], ALU.mult).then_inc(S["mix_g"], 1)

            def x1_stats(t):
                m = xst[:, t % 2, :]
                g.wait_ge(S["x1_st"], t + 1)
                own(g.tensor_scalar(m[:, 2:3], m[:, 1:2], EPS, None, ALU.add))
                own(g.tensor_tensor(m[:, 3:4], m[:, 2:3], halfpow[:, 0:1], ALU.pow))
                g.tensor_scalar(m[:, 4:5], m[:, 0:1], m[:, 3:4], -1.0, ALU.mult, ALU.mult).then_inc(S["x1_p"], 1)

            def quantise_low(i):
                g.wait_ge(S["wr_thr"], i + 1)
                g.wait_ge(S[f"wr_in{i % 2}"], 48 * (i // 2 + 1))
                if i == 1:
                    g.wait_ge(S["wr_q"], i)
                if i >= 2:
                    g.wait_ge(S["wr_q"], i - 1)
                if i == 0:
                    g.wait_ge(S["kmT_mm"], 1)
                low = wb_first if i < 2 else wb[i % 2]
                th = gthr[:, i % 2, :, :]
                for j in range(12 if i < 2 else POOL_GROUPS):
                    ins = g.tensor_scalar(low[:, j, :], wraw[:, i % 2, j, :], th[:, 2, j:j + 1], th[:, 0, j:j + 1], ALU.is_lt, ALU.mult)
                ins.then_inc(S["wr_b"], 1)
                g.wait_ge(S["wr_b"], i + 1)
                g.wait_ge(S["wr_a"], i + 1)
                g.tensor_tensor(wa[:, i % 2, :, :], wa[:, i % 2, :, :], low, ALU.subtract).then_inc(S["wr_q"], 1)

            quantise_low(0)
            quantise_low(1)
            g.wait_ge(S["gain_in"], 16)
            for t in range(NT + 2):
                if t < NT:
                    mix_stats(t)
                if 1 <= t <= NT:
                    mix_gain(t - 1)
                if t >= 2:
                    x1_stats(t - 2)
            for i in range(2, FT):
                quantise_low(i)

        @block.tensor
        def _(pe):
            def triple(to, stat, mov, pairs, first=True, last=True):
                n, total = 0, 3 * len(pairs)
                for p in pairs:
                    for a, m in PARTS:
                        ins = pe.matmul(to, stat(a, p), mov(m, p), start=first and n == 0, stop=last and n == total - 1)
                        n += 1
                return ins

            def turn_x(t):
                pe.wait_ge(S["xn_ready"], t + 1)
                if t:
                    pe.wait_ge(S["xT_lo"], t)
                for k in range(K):
                    ins = pe.transpose(bank[5][:, k * P:(k + 1) * P], xn[:, t % 2, k * 128:(k + 1) * 128], ident[0:P, 0:P])
                ins.then_inc(S["xT_done"], 1)

            pe.wait_ge(S["g_ident"], 2)
            pe.wait_ge(S["bound_v"], 1)
            for a in range(2):
                for h in range(2):
                    at = (a * 2 + h) * ROWS
                    ins = pe.transpose(bank[0][0:NB, at:at + ROWS], ov[:, h, 2 + a, :], ident[0:ROWS, 0:ROWS])
            ins.then_inc(S["bT_mm"], 1)
            pe.wait_ge(S["edge_k"], 1)
            for h in range(2):
                for a in range(2):
                    ins = pe.transpose(bank[4 - h][0:P, a * ROWS:(a + 1) * ROWS], edges[:, a, h, :], ident[0:ROWS, 0:ROWS])
            ins.then_inc(S["bT_mm"], 1)
            pe.wait_ge(S["bound_v"], 2)
            for a in range(2):
                ins = pe.transpose(bank[1][0:1, a * NB:(a + 1) * NB], bounds[:, a:a + 1], ident[0:NB, 0:NB])
            ins.then_inc(S["bp_mm"], 1)
            pe.wait_ge(S["small_in"], 32)
            pe.transpose(bank[2][:, 0:K], grow[:], ident[0:K, 0:K]).then_inc(S["gT_mm"], 1)
            pe.wait_ge(S["brow_d"], 1)
            pe.wait_ge(S["gcol_d"], 1)
            pe.nop().then_inc(S["ex_used"], GRP)
            over = pe.value_load(brow[0:1, 2 * NB:2 * NB + 1], min_val=0, max_val=1)
            visit = pe.alloc_register("pe_visit")
            pe.reg_mov(visit, 0)

            def prep(n):
                g = n // K
                pe.wait_ge(S[f"raw_in{g % 2}"], 16 * (g // 2 + 2))
                if n:
                    pe.wait_ge(S["prep_out"], n)
                for j in range(4):
                    ins = pe.transpose(bank[4][:, j * 128:(j + 1) * 128], raw[:, g % 2, j, n % K * 128:(n % K + 1) * 128], ident[:])
                ins.then_inc(S["prep_T"], 1)

            def count(b):
                if b >= 2:
                    pe.wait_ge(S["cs_out"], b - 1)
                extra, lo, more = bound[b]
                to = bank[b % 2][0:P, 0:NT * SPAN]
                half, other = b % 2, 1 - b % 2
                for q in range(MOST):
                    pe.wait_ge(S["oh_ready"], b * MOST + q + 1)
                    pe.matmul(to, oh_lane[half][:, q, 0:P], oh_key[:, half * MOST + q, :], start=q == 0, stop=True, skip_group_check=True)
                with pe.If_ne(more, 0):
                    with pe.Fori(lo + MOST, lo + (extra + MOST), GRP):
                        w = pe.snap(visit, min_val=0, max_val=NB * (NCH + GRP))
                        for q in range(GRP):
                            pe.wait_ge(S["ex_ready"], w + (q + 1))
                            pe.matmul(to, oh_lane[other][:, q, 0:P], oh_key[:, other * MOST + q, :], start=False, stop=True, skip_group_check=True).then_inc(S["ex_used"], 1)
                        pe.reg_add(visit, visit, GRP)
                pe.matmul(bank[b % 2][0:1, 511:512], ones_h[:], ones_h[:], start=False, stop=True, skip_group_check=True).then_inc(S["cnt_mm"], 1)

            bound = {}

            def turn_counts(n):
                m, d = piece(n)
                pair, e = m // 2, slice(m % 2 * P, m % 2 * P + P)
                pe.wait_ge(S["cs_lo"], PAIR * (pair + 1))
                if n >= 2:
                    pe.wait_ge(S["t_out"], n - 1)
                for u in range(d.start // P, d.stop // P):
                    to = bank[2 + n % 2][0:P, u * P - d.start:(u + 1) * P - d.start]
                    pe.matmul(to, cs_hi[pair % 2][:, u, e], ident_h[0:P, 0:P], start=True, stop=False)
                    ins = pe.matmul(to, cs_lo[pair % 2][:, u, e], ident_h[0:P, 0:P], start=False, stop=True)
                ins.then_inc(S["t_mm"], 1)

            def product(b, t, w, c0, done):
                triple(b[0:P, :], lambda a, k: qT[:, a, k, t * P:(t + 1) * P], lambda m, k: w[:, m, k, c0:c0 + D], range(K)).then_inc(done, 1)

            for b in range(NB):
                if b % AHEAD == 0:
                    bound.update(bounds_at(pe, b))
                count(b)
                if b == 0:
                    turn_x(0)
                for t in tile_at(b, AT_TURN):
                    turn_x(t)
                for n in preps_at(b):
                    prep(n)
                for n in pieces_at(b):
                    turn_counts(n)
                for t in tile_at(b, AT_PRODUCT):
                    pe.wait_ge(S["xT_lo"], t + 1)
                    if t:
                        pe.wait_ge(S["acc_done"], t)
                    else:
                        pe.wait_ge(S["wcn_lo"], 1)
                    product(bank[7], t, wcn, 0, S["alpha_mm"])
                    if t:
                        pe.wait_ge(S["beta_lo"], t)
                    else:
                        pe.wait_ge(S["wcn_lo"], 2)
                    product(bank[6], t, wcn, D, S["beta_mm"])

            def tail(n):
                for at in TAIL[n]:
                    (turn_counts if at[0] else prep)(at[1])

            def turn_q(t):
                pe.wait_ge(S["q_norm"], t + 1)
                if t:
                    pe.wait_ge(S["qT_lo"], t)
                else:
                    pe.wait_ge(S["t_out"], 3 * NT)
                for k in range(K):
                    ins = pe.transpose(bank[2][:, k * P:(k + 1) * P], qn[:, k * 128:(k + 1) * 128], ident[0:P, 0:P])
                ins.then_inc(S["qT_mm"], 1)

            pe.wait_ge(S["prep_lo"], 3 * K)
            for t in range(NT):
                if t == 0:
                    pe.wait_ge(S["beta_lo"], NT)
                elif t == 1:
                    pe.wait_ge(S["acc_done"], NT)
                else:
                    pe.wait_ge(S["q_sub"], t - 1)
                product(bank[6 + t % 2], t, wqkvT, 0, S["q_mm"])
                if t == 0:
                    tail(0)
                if t < 2:
                    pe.wait_ge(S["cs_out"], NB)
                else:
                    pe.wait_ge(S["k_out"], t - 1)
                product(bank[t % 2], t, wqkvT, D, S["k_mm"])
                if t == 0:
                    tail(1)
                else:
                    turn_q(t - 1)
                if t == 1:
                    pe.wait_ge(S["prep_out"], 4 * K)
                if t >= 2:
                    pe.wait_ge(S["v_lo"], t - 1)
                product(bank[5 - t % 2], t, wqkvT, 2 * D, S["v_mm"])
                if t == 0:
                    tail(2)
            pe.wait_ge(S["q_sub"], NT)
            pe.wait_ge(S["kmax_d"], NT)
            for k in range(K):
                ins = pe.transpose(bank[7][:, k * P:(k + 1) * P], kmax[:, k * 128:(k + 1) * 128], ident[0:P, 0:P])
            ins.then_inc(S["kmT_mm"], 1)
            pe.wait_ge(S["t_lo"], 3 * NT)
            pe.wait_ge(S["q_sub"], NT)
            for u in range(NT):
                for m in range(NT):
                    pe.matmul(bank[6][0:P, u:u + 1], counts[:, m, u * P:(u + 1) * P], ones_h[:], start=m == 0, stop=m == NT - 1, skip_group_check=True)
            with pe.If(over):
                for u in range(NT):
                    for m in range(NT):
                        pe.matmul(bank[6][0:P, u:u + 1], counts[:, m, u * P:(u + 1) * P], ones_h[:], start=m == 0, stop=False, skip_group_check=True)
                        pe.matmul(bank[6][0:P, u:u + 1], counts_lo[:, m, u * P:(u + 1) * P], ones_h[:], start=False, stop=m == NT - 1, skip_group_check=True)
            pe.matmul(bank[6][0:1, 511:512], ones_h[:], ones_h[:], start=False, stop=True, skip_group_check=True).then_inc(S["cn_mm"], 1)
            pe.wait_ge(S["kmc_d"], 1)
            for k in range(K):
                ins = pe.matmul(bank[7][0:P, k * 128:(k + 1) * 128], kmaxc[:, k:k + 1].broadcast_to([128, P]), ident[:], start=True, stop=True)
            ins.then_inc(S["kmb_mm"], 1)
            turn_q(NT - 1)

            def gamma(t):
                if t >= 2:
                    pe.wait_ge(S["gam_d"], t - 1)
                to = bank[t % 2][0:P, :]
                for m in range(NT):
                    for c in range(2):
                        if m == NT - 1 and c == 1:
                            with pe.If(over):
                                for o in range(NT):
                                    pe.matmul(to, counts_lo[:, o, t * P:(t + 1) * P], betas[:, 0, o, :], start=False, stop=False)
                        ins = pe.matmul(to, counts[:, m, t * P:(t + 1) * P], betas[:, c, m, :], start=m == 0 and c == 0, stop=m == NT - 1 and c == 1)
                ins.then_inc(S["gam_mm"], 1)

            def mix(t):
                if t >= 2:
                    pe.wait_ge(S["mix_n"], t - 1)
                triple(bank[2 + t % 2][0:P, :], lambda a, k: qT[:, a, k, t * P:(t + 1) * P], lambda m, k: w2[:, m, k, :], range(K)).then_inc(S["mix_mm"], 1)

            def turn_x1(t):
                pe.wait_ge(S["x2_n"], t + 1)
                if t >= 2:
                    pe.wait_ge(S["x2_lo"], t - 1)
                for k in range(K):
                    ins = pe.transpose(bank[4 + t % 2][:, k * P:(k + 1) * P], xn2[:, t % 2, k * 128:(k + 1) * 128], ident[0:P, 0:P])
                ins.then_inc(S["x2T_mm"], 1)

            pe.wait_ge(S["k_out"], NT)
            for t in range(3):
                gamma(t)
            pe.wait_ge(S["v_one"], 2)
            pe.wait_ge(S["v_lo"], NT)
            pe.wait_ge(S["q_sub"], NT)
            pe.wait_ge(S["qT_lo"], NT)
            for t in range(NT):
                pe.wait_ge(S["ek_lo"], t + 1)
                for k in range(K):
                    ins = triple(bank[2 + k][:, 0:129], lambda a, p: ek[:, t, a, k * 128:(k + 1) * 128], lambda m, p: vp[:, m, t, k, 0:129],
                                 [0], t == 0, t == NT - 1)
            ins.then_inc(S["ctx_mm"], 1)
            gamma(3)
            pe.wait_ge(S["k_sub"], NT)
            for k in range(K):
                pe.wait_ge(S["ctx_n"], k + 1)
                if k == 0:
                    pe.wait_ge(S["crec_d"], 1)
                pe.transpose(bank[6][:, 0:128], ctxn[:, k % 2, :], ident[:]).then_inc(S["ctxT_mm"], 1)
                gamma(4 + k)
                pe.wait_ge(S["ctx_lo"], k + 1)
                if k:
                    pe.wait_ge(S["w2_lo"], k)
                triple(bank[7][:, :], lambda a, p: ctxT[:, k % 2, a, :], lambda m, p: woutT[:, m, k, :], [0]).then_inc(S["w2_mm"], 1)
            gamma(8)
            pe.wait_ge(S["w2_lo"], K)

            def turn_w(i, g, half, done):
                pe.wait_ge(S["wr_q"], i + 1)
                b = (3 * half + g) % 2
                if done is not None:
                    pe.wait_ge(S["wr_lo"], done)
                for k in range(K):
                    ins = pe.transpose(bank[6 + b][:, k * 128:(k + 1) * 128], wa[:, half, 4 * g + k, :], ident[:])
                ins.then_inc(S["wr_T"], 1)

            for t in range(NT):
                mix(t)
                if t == 1:
                    gamma(9)
                if t >= 4:
                    turn_x1(t - 4)
                if 2 <= t < 8:
                    n = t - 2
                    turn_w(n // 3, n % 3, n // 3, n - 1 if n >= 2 else None)

            def gate_up(i, half, u, turn=True, first=False):
                pe.wait_ge(S["wr_lo"], u + 2)
                for c, (n0, nn) in enumerate(NC3):
                    if first:
                        pe.wait_ge(S["x2_lo"], TILES_OF[c])
                    else:
                        pe.wait_ge(S["hf_d"], u + (c - 2))
                    for z in range(2):
                        if first and c < 2:
                            turn_x1(NT - 4 + 2 * c + z)
                        ins = triple(bank[2 * c + z][:, 0:nn], lambda a, k: wgu[:, half, a, (z * K + k) * 128:(z * K + k + 1) * 128],
                                     lambda m, k: qT[:, m, k, n0:n0 + nn], range(K))
                    ins.then_inc(S["gu_mm"], 1)
                    if turn:
                        turn_w(i + 1, c, 1 - half, u + (3 + c - 1))

            gate_up(0, 0, 0, turn=False, first=True)
            with pe.Fori(1, FT - 2, 2) as i:
                for e in range(2):
                    gate_up(i + e, (1 + e) % 2, i * 3 + 3 * e)
            gate_up(FT - 2, 1, 3 * (FT - 2))
            gate_up(FT - 1, 0, 3 * (FT - 1), turn=False)

            def down(t, half):
                triple(bank[half][0:P, :], lambda a, i: hT[:, a, i, bass.ds(t * P, P)], lambda m, i: wdT[:, m, i, :], range(FT)).then_inc(S["dn_mm"], 1)

            pe.wait_ge(S["wr_lo"], 3 * FT)
            for t in range(2):
                pe.wait_ge(S["h_lo"], 3 * FT - 2)
                down(t, t)
            pe.wait_ge(S["h_lo"], 3 * FT)
            with pe.Fori(1, NT // 2) as two:
                for e in range(2):
                    pe.wait_ge(S["dn_d"], two * 2 + (e - 1))
                    down(two * 2 + e, e)

        @block.scalar
        def _(s):
            def prep_out(n):
                g, k = n // K, n % K
                s.wait_ge(S["prep_T"], n + 1)
                if n >= 2:
                    s.wait_ge(S["prep_lo"], n - 1)
                if n == 3 * K:
                    s.wait_ge(S["t_mm"], PIECES * 4)
                by = gcol[:, k:k + 1] if g < 3 else W_SCALE
                to = wqkvT[:, 0, k, g * D:(g + 1) * D] if g < 3 else woutT[:, 0, k, :]
                s.activation(to, bank[4][:, :], ACT.Copy, scale=by)
                s.activation(stage_w[:, n % 2, :], bank[4][:, :], ACT.Copy, scale=by).then_inc(S["prep_out"], 1)

            def span_out(b):
                s.wait_ge(S["cnt_mm"], b + 1)
                if b:
                    s.wait_ge(S["cs_lo"], b)
                if b % PAIR == 0 and b >= 2 * PAIR:
                    s.wait_ge(S["t_mm"], PIECES * (b // PAIR - 1))
                p = bank[b % 2][0:P, 0:NT * SPAN]
                s.activation(cs_hi[b // PAIR % 2][:, :, b % PAIR * SPAN:(b % PAIR + 1) * SPAN], p.rearrange("p (u d) -> p u d", u=NT), ACT.Copy)
                s.activation(stage_c, p, ACT.Copy).then_inc(S["cs_out"], 1)

            def piece_out(n):
                s.wait_ge(S["t_mm"], n + 1)
                if n > PIECES * (NB // PAIR - 1):
                    s.wait_ge(S["t_lo"], n - 1)
                    s.wait_ge(S["cs_lo"], NB)
                elif n:
                    s.wait_ge(S["t_lo"], n)
                m, d = piece(n)
                p = bank[2 + n % 2][0:P, 0:d.stop - d.start]
                s.activation(counts[:, m, d], p, ACT.Copy)
                s.activation(staged(n)[:, 0:d.stop - d.start], p, ACT.Copy).then_inc(S["t_out"], 1)

            def norm(t):
                s.wait_ge(S["r_ready"], min(t // 2 + 1, 3))
                if t >= 2:
                    s.wait_ge(S["xT_done"], t - 1)
                s.activation(xn[:, t % 2, :], xr[:, t, :], ACT.Identity, bias=nmean[:, t:t + 1], scale=rstd[:, t:t + 1]).then_inc(S["xn_ready"], 1)

            def xT_high(t):
                s.wait_ge(S["xT_done"], t + 1)
                s.activation(qT[:, 0, :, t * P:(t + 1) * P], tiles(bank[5]), ACT.Copy, scale=X_SCALE).then_inc(S["xT_hi"], 1)

            def wcn_high(i):
                s.wait_ge(S[f"raw_in{i}"], 16)
                s.activation(wcn[:, 0, :, i * D:(i + 1) * D], raw[:, i, :, :], ACT.Copy, scale=W_SCALE).then_inc(S["wcn_own"], 1)
                s.wait_ge(S["wcn_own"], i + 1)
                s.activation(raw[:, i, :, :], raw[:, i, :, :], ACT.Copy, scale=W_SCALE).then_inc(S["wcn_hi"], 1)

            norm(0)
            norm(1)
            wcn_high(0)
            s.wait_ge(S["gcol_d"], 1)
            for b in range(NB):
                if b == 0:
                    xT_high(0)
                    wcn_high(1)
                span_out(b)
                for t in tile_at(b + 1, AT_TURN):
                    if t >= 2:
                        norm(t)
                for t in tile_at(b, AT_TURN):
                    xT_high(t)
                for n in preps_at(b):
                    prep_out(n)
                for n in pieces_at(b):
                    piece_out(n)
                for t in tile_at(b, AT_PRODUCT):
                    s.wait_ge(S["beta_mm"], t + 1)
                    s.activation(betas[:, 0, t, :], bank[6][0:P, :], ACT.Copy, scale=1.0 / W_SCALE).then_inc(S["beta_hi"], 1)

            def tail(n):
                for at in TAIL[n]:
                    (piece_out if at[0] else prep_out)(at[1])

            s.wait_ge(S["r2_ready"], 3)
            tail(0)
            for t in range(NT):
                s.wait_ge(S["q_sub"], t + 1)
                s.activation(qe, qe, ACT.Exp, scale=r2k[:, t:t + 1]).then_inc(S["q_exp"], 1)
                if t == 0:
                    tail(1)
                s.wait_ge(S["k_mm"], t + 1)
                if t == 8:
                    s.wait_ge(S["prep_lo"], 4 * K)
                s.activation(kf[:, t, :], bank[t % 2][0:P, :], ACT.Copy, scale=r2k[:, t:t + 1]).then_inc(S["k_out"], 1)
                if t == 0:
                    tail(2)
                if t:
                    s.wait_ge(S["qT_mm"], t)
                    s.activation(qT[:, 0, :, (t - 1) * P:t * P], tiles(bank[2]), ACT.Copy, scale=Q_SCALE).then_inc(S["qT_hi"], 1)
                s.wait_ge(S["v_mm"], t + 1)
                s.activation(vp[:, 0, t, :, 0:128], bank[5 - t % 2][0:P, :].rearrange("p (k e) -> p k e", k=K), ACT.Copy, scale=r2v[:, t:t + 1]).then_inc(S["v_hi"], 1)
            s.wait_ge(S["qT_mm"], NT)
            s.activation(qT[:, 0, :, (NT - 1) * P:NT * P], tiles(bank[2]), ACT.Copy, scale=Q_SCALE).then_inc(S["qT_hi"], 1)
            for t in range(NT):
                s.wait_ge(S["k_sub"], t + 1)
                if t >= 2:
                    s.wait_ge(S["ek_lo"], t - 1)
                s.activation(ering[:, t % 2, :], kf[:, t, :], ACT.Exp).then_inc(S["k_exp"], 1)
                s.wait_ge(S["k_exp"], t + 1)
                s.activation(ek[:, t, 0, :], ering[:, t % 2, :], ACT.Copy).then_inc(S["ek_hi"], 1)
            s.wait_ge(S["ctx_zero"], 1)
            for k in range(K):
                s.wait_ge(S["ctxT_mm"], k + 1)
                if k >= 2:
                    s.wait_ge(S["w2_mm"], k - 1)
                for h in range(2):
                    d = slice(64 * h, 64 * h + 64)
                    ins = s.activation(ctxT[d, k % 2, 0, d], bank[6][d, d], ACT.Copy, scale=C_SCALE)
                ins.then_inc(S["ctx_hi"], 1)
                s.wait_ge(S["w2_mm"], k + 1)
                s.activation(w2[:, 0, k, :], bank[7][:, :], ACT.Copy, scale=1.0 / W_SCALE).then_inc(S["w2_hi"], 1)

            def mix_out(t):
                m = mst[:, t % 2, :]
                s.wait_ge(S["mst_p"], t + 1)
                if t >= 2:
                    s.wait_ge(S["x1_d"], t - 1)
                s.activation(xn[:, t % 2, :], bank[2 + t % 2][0:P, :], ACT.Identity, bias=m[:, 5:6], scale=m[:, 4:5]).then_inc(S["mix_n"], 1)

            def x1_norm(t):
                s.wait_ge(S["x1_p"], t + 1)
                if t >= 2:
                    s.wait_ge(S["x2T_mm"], t - 1)
                s.activation(xn2[:, t % 2, :], xr[:, t, :], ACT.Identity, bias=xst[:, t % 2, 4:5], scale=xst[:, t % 2, 3:4]).then_inc(S["x2_n"], 1)

            def x2_high(t):
                s.wait_ge(S["x2T_mm"], t + 1)
                s.activation(qT[:, 0, :, t * P:(t + 1) * P], tiles(bank[4 + t % 2]), ACT.Copy, scale=X_SCALE).then_inc(S["x2_hi"], 1)

            def w_high(i, g, half, u, reused=True):
                s.wait_ge(S["wr_T"], u + (g + 1))
                if g < 2 and reused:
                    s.wait_ge(S["gu_mm"], u - 3)
                to = wgu[:, half, 0, g * D:(g + 1) * D] if g < 2 else hidden(wdT, 0, i)
                s.activation(to, bank[6 + (3 * half + g) % 2][:, :], ACT.Copy, scale=W_SCALE).then_inc(S["wr_hi"], 1)

            for t in range(NT):
                mix_out(t)
                if t >= 3:
                    x1_norm(t - 3)
                if t >= 4:
                    x2_high(t - 4)
                if 2 <= t < 8:
                    i = (t - 2) // 3
                    w_high(i, (t - 2) % 3, i, 3 * i, reused=False)
            x1_norm(NT - 3)
            x2_high(NT - 4)
            x1_norm(NT - 2)
            x2_high(NT - 3)
            x1_norm(NT - 1)

            def gated(i, half, u, turn=True, first=False):
                for c, (n0, nn) in enumerate(NC3):
                    if first and c == 1:
                        x2_high(NT - 2)
                        x2_high(NT - 1)
                    slot = (half + c) % 2
                    s.wait_ge(S["gu_mm"], u + (c + 1))
                    if not first or c == 2:
                        s.wait_ge(S["hf_d"], u + (c - 1))
                    s.activation(sg[:, slot, 0:nn], bank[2 * c][:, 0:nn], ACT.Silu, scale=UNDO).then_inc(S["sg_d"], 1)
                    s.wait_ge(S["hf_d"], u + (c + 1))
                    s.activation(hidden(hT, 0, i)[:, n0:n0 + nn], hf[:, slot, 0:nn], ACT.Copy).then_inc(S["h_hi"], 1)
                    if turn:
                        w_high(i + 1, c, 1 - half, u + 3)

            gated(0, 0, 0, turn=False, first=True)
            with s.Fori(1, FT - 2, 2) as i:
                for e in range(2):
                    gated(i + e, 1 - e, i * 3 + 3 * e)
            gated(FT - 2, 1, 3 * (FT - 2))
            gated(FT - 1, 0, 3 * (FT - 1), turn=False)

        @block.vector
        def _(v):
            n_own = [0]

            def own(ins):
                n_own[0] += 1
                ins.then_inc(S["v_own"], 1)
                v.wait_ge(S["v_own"], n_own[0])

            def qT_low(t):
                v.wait_ge(S["qT_hi"], t + 1)
                d = slice(t * P, (t + 1) * P)
                v.scalar_tensor_tensor(qT[:, 1, :, d], tiles(bank[2]), Q_SCALE, qT[:, 0, :, d], ALU.mult, ALU.subtract).then_inc(S["qT_lo"], 1)

            def stats(t):
                v.wait_ge(S[f"x_in{t // 2}"], 16)
                own(v.bn_stats(st6[:, t, :], xr[:, t, :]))
                v.bn_aggr(mv[:, t, :], st6[:, t, :]).then_inc(S["stats_v"], 1)

            v.wait_ge(S["edge_in"], 32)
            v.tensor_copy(edges.rearrange("r a h e -> r a (h e)"), edges_i).then_inc(S["edge_f"], 1)
            v.wait_ge(S["edge_f"], 1)
            own(v.tensor_reduce(ext[:, 0, :], edges[:, 1, :, :], AX.X, ALU.max))
            own(v.tensor_reduce(ext[:, 1, :], edges[:, 1, :, :], AX.X, ALU.min))
            own(v.tensor_scalar(ext[:, 1, :], ext[:, 1, :], float(SPAN - 1), None, ALU.subtract))
            v.wait_ge(S["g_const"], 10)
            for h in range(2):
                own(v.tensor_scalar(ov[:, h, 0, :], block_at[:], ext[:, 0, h:h + 1], None, ALU.is_le))
                own(v.tensor_scalar(ov[:, h, 1, :], block_at[:], ext[:, 1, h:h + 1], None, ALU.is_ge))
                own(v.tensor_tensor(ov[:, h, 0, :], ov[:, h, 0, :], ov[:, h, 1, :], ALU.mult))
                v.tensor_scalar(ov[:, h, 2, :], ov[:, h, 0, :], chunk_up[:, h:h + 1], None, ALU.mult)
                ins = v.tensor_scalar(ov[:, h, 3, :], ov[:, h, 0, :], chunk_dn[:, h:h + 1], None, ALU.mult)
            ins.then_inc(S["bound_v"], 1)
            src_f, dst_f = [edges[:, a, :, :].rearrange("r h e -> r (h e)") for a in range(2)]
            whole = 1.5 * 2 ** 23
            own(v.tensor_scalar(tile_of[:, 0, :], src_f, 1.0 / P, -0.5 + 0.5 / P, ALU.mult, ALU.add))
            own(v.tensor_scalar(tile_of[:, 1, :], tile_of[:, 0, :], whole, None, ALU.add))
            own(v.tensor_scalar(tile_of[:, 0, :], tile_of[:, 1, :], whole, None, ALU.subtract))
            v.scalar_tensor_tensor(src_f, tile_of[:, 0, :], -float(P), src_f, ALU.mult, ALU.add)
            v.scalar_tensor_tensor(dst_f, dst_f, float(NT), tile_of[:, 0, :], ALU.mult, ALU.add).then_inc(S["edge_k"], 1)
            v.wait_ge(S["bT_mm"], 1)
            own(v.tensor_reduce(bounds[:, 0:2], bank[0][0:NB, 0:4 * ROWS].rearrange("p (a j) -> p a j", a=2), AX.X, ALU.max))
            own(v.tensor_scalar(bounds[:, 1:2], bounds[:, 1:2], -1.0, float(NCH), ALU.mult, ALU.add))
            own(v.tensor_tensor(bounds[:, 2:3], bounds[:, 0:1], bounds[:, 1:2], ALU.subtract))
            v.tensor_scalar(bounds[:, 0:1], bounds[:, 2:3], float(MOST), 0.0, ALU.subtract, ALU.max).then_inc(S["bound_v"], 1)
            v.wait_ge(S["bT_mm"], 2)
            for h in range(2):
                for a in range(2):
                    ins = v.tensor_copy((e_lane, e_key)[a][:, h:NCH:2], bank[4 - h][0:P, a * ROWS:(a + 1) * ROWS])
            own(ins)
            v.wait_ge(S["bp_mm"], 1)
            row = bank[1][0:1, 0:2 * NB]
            own(v.tensor_copy(brow[:, 0:2 * NB].rearrange("o (b a) -> o a b", a=2), row.rearrange("o (a b) -> o a b", a=2)))
            own(v.tensor_reduce(span[:, 0:1], row[:, 0:NB], AX.X, ALU.max))
            v.tensor_scalar(brow[:, 2 * NB:2 * NB + 1], span[:, 0:1], float(2048 // P - MOST), None, ALU.is_gt).then_inc(S["brow_d"], 1)
            stats(0)
            stats(1)
            v.wait_ge(S["gT_mm"], 1)
            v.tensor_scalar(gcol[:], bank[2][:, 0:K], W_SCALE, None, ALU.mult).then_inc(S["gcol_d"], 1)
            v.wait_ge(S["brow_d"], 1)
            visit = v.alloc_register("dve_visit")
            v.reg_mov(visit, 0)

            def onehots(b, half, q, chunk, done):
                v.tensor_scalar(oh_key[:, half * MOST + q, :], iota_key[:], e_key[:, bass.ds(chunk, 1)], -float(b * NT * SPAN), ALU.subtract, ALU.is_equal)
                v.tensor_scalar(oh_lane[half][:, q, 0:P], iota_lane[:, 0:P], e_lane[:, bass.ds(chunk, 1)], None, ALU.is_equal).then_inc(done, 1)

            end = v.alloc_register("dve_end")

            def count(b):
                extra, lo, more = bound[b]
                if b >= 2:
                    v.wait_ge(S["cnt_mm"], b - 1)
                for q in range(MOST):
                    onehots(b, b % 2, q, lo + q, S["oh_ready"])
                with v.If_ne(more, 0):
                    if b >= 1:
                        v.wait_ge(S["cnt_mm"], b)
                    v.reg_mov(end, lo + (extra + MOST))
                    with v.Fori(lo + MOST, v.snap(end, min_val=MOST + 1, max_val=NCH), GRP) as j:
                        w = v.snap(visit, min_val=0, max_val=NB * (NCH + GRP))
                        for q in range(GRP):
                            if q % 2 == 0:
                                v.wait_ge(S["ex_used"], w + (q + 2))
                            onehots(b, 1 - b % 2, q, j + q, S["ex_ready"])
                        v.reg_add(visit, visit, GRP)
                    v.wait_ge(S["cnt_mm"], b + 1)

            def xT_low(t):
                v.wait_ge(S["xT_hi"], t + 1)
                d = slice(t * P, (t + 1) * P)
                v.scalar_tensor_tensor(qT[:, 1, :, d], tiles(bank[5]), X_SCALE, qT[:, 0, :, d], ALU.mult, ALU.subtract).then_inc(S["xT_lo"], 1)

            bound = {}
            for b in range(NB):
                if b % AHEAD == 0:
                    bound.update(bounds_at(v, b))
                count(b)
                if 2 * b + 3 < NT:
                    stats(2 * b + 2)
                    stats(2 * b + 3)
                for t in tile_at(b, AT_PRODUCT):
                    xT_low(t)
                for t in tile_at(b, AT_BETA):
                    v.wait_ge(S["beta_hi"], t + 1)
                    v.scalar_tensor_tensor(betas[:, 1, t, :], bank[6][0:P, :], 1.0 / W_SCALE, betas[:, 0, t, :], ALU.mult, ALU.subtract).then_inc(S["beta_lo"], 1)
                    v.wait_ge(S["alpha_mm"], t + 1)
                    v.wait_ge(S["xb_done"], t + 1)
                    v.scalar_tensor_tensor(xr[:, t, :], bank[7][0:P, :], UNDO, xr[:, t, :], ALU.mult, ALU.add).then_inc(S["acc_done"], 1)

            heads = lambda ap: ap.rearrange("p (h d) -> p h d", d=HEAD)
            spread = lambda ap: ap.rearrange("p (h o) -> p h o", o=1).broadcast_to([P, HEADS, HEAD])
            v.wait_ge(S["xT_done"], NT)
            for t in range(NT):
                qb = heads(bank[6 + t % 2][0:P, :])
                v.wait_ge(S["q_mm"], t + 1)
                v.tensor_reduce(qmx[:], qb, AX.X, ALU.max).then_inc(S["q_max"], 1)
                v.wait_ge(S["q_max"], t + 1)
                if t:
                    v.wait_ge(S["q_norm"], t)
                v.tensor_tensor(heads(qe), qb, spread(qmx[:]), ALU.subtract).then_inc(S["q_sub"], 1)
                v.wait_ge(S["k_out"], t + 1)
                if t == 0:
                    v.tensor_copy(kmax, kf[:, 0, :]).then_inc(S["kmax_d"], 1)
                else:
                    v.wait_ge(S["kmax_d"], t)
                    v.tensor_tensor(kmax, kmax, kf[:, t, :], ALU.max).then_inc(S["kmax_d"], 1)
                v.wait_ge(S["q_exp"], t + 1)
                v.tensor_reduce(qsum[:], heads(qe), AX.X, ALU.add).then_inc(S["q_sum"], 1)
                v.wait_ge(S["q_sum"], t + 1)
                v.reciprocal(qsum[:], qsum[:]).then_inc(S["q_rec"], 1)
                v.wait_ge(S["q_rec"], t + 1)
                if t:
                    v.wait_ge(S["qT_mm"], t)
                v.tensor_tensor(heads(qn), heads(qe), spread(qsum[:]), ALU.mult).then_inc(S["q_norm"], 1)
                if t:
                    qT_low(t - 1)
                v.wait_ge(S["v_hi"], t + 1)
                if t == 0:
                    v.wait_ge(S["cnt_mm"], NB)
                if t == 5:
                    v.wait_ge(S["t_lo"], 3 * NT)
                v.scalar_tensor_tensor(vp[:, 1, t, :, 0:128], bank[5 - t % 2][0:P, :].rearrange("p (k e) -> p k e", k=K), r2v[:, t:t + 1], vp[:, 0, t, :, 0:128], ALU.mult, ALU.subtract).then_inc(S["v_lo"], 1)
            v.wait_ge(S["kmT_mm"], 1)
            v.tensor_reduce(kmaxc[:], tiles(bank[7]), AX.X, ALU.max).then_inc(S["kmc_d"], 1)

            def gamma_out(t):
                v.wait_ge(S["gam_mm"], t + 1)
                v.wait_ge(S["acc_done"], t + 1)
                if t == 0:
                    v.wait_ge(S["crec_d"], 1)
                v.scalar_tensor_tensor(xr[:, t, :], bank[t % 2][0:P, :], crec[:, t:t + 1], xr[:, t, :], ALU.mult, ALU.add).then_inc(S["gam_d"], 1)

            def group_scales(i, half, reused=True):
                th = gthr[:, half, :, :]
                v.wait_ge(S[f"wr_in{half}"], i * 24 + (24 if half else 48))
                v.tensor_reduce(gsum[:, half, :], wraw[:, half, :, :], AX.X, ALU.add, apply_absolute_value=True).then_inc(S["wr_abs"], 1)
                v.wait_ge(S["wr_abs"], i + 1)
                if reused:
                    v.wait_ge(S["wr_b"], i - 1)
                v.tensor_scalar(th[:, 0, :], gsum[:, half, :], 1.0 / 128, EPS, ALU.mult, ALU.add).then_inc(S["wr_scale"], 1)
                v.wait_ge(S["wr_scale"], i + 1)
                v.tensor_scalar(th[:, 1, :], th[:, 0, :], 0.5, None, ALU.mult)
                v.tensor_scalar(th[:, 2, :], th[:, 0, :], -0.5, None, ALU.mult).then_inc(S["wr_thr"], 1)

            def quantise_high(i, half, reused=True):
                th = gthr[:, half, :, :]
                v.wait_ge(S["wr_thr"], i + 1)
                if reused:
                    v.wait_ge(S["wr_T"], i * 3 - 3)
                for j in range(12):
                    ins = v.tensor_scalar(wa[:, half, j, :], wraw[:, half, j, :], th[:, 1, j:j + 1], th[:, 0, j:j + 1], ALU.is_gt, ALU.mult)
                if reused:
                    v.wait_ge(S["wr_q"], i - 1)
                    for j in range(POOL_GROUPS, 12):
                        ins = v.tensor_scalar(wb[half][:, j, :], wraw[:, half, j, :], th[:, 2, j:j + 1], th[:, 0, j:j + 1], ALU.is_lt, ALU.mult)
                ins.then_inc(S["wr_a"], 1)

            v.wait_ge(S["kmb_mm"], 1)
            for t in range(NT):
                v.tensor_tensor(kf[:, t, :], kf[:, t, :], bank[7][0:P, :], ALU.subtract).then_inc(S["k_sub"], 1)
                if t == 2:
                    qT_low(NT - 1)
            v.wait_ge(S["cn_mm"], 1)
            own(v.reciprocal(crec[:], bank[6][0:P, 0:NT]))
            v.tensor_scalar(crec[:], crec[:], 1.0 / X_SCALE, None, ALU.mult).then_inc(S["crec_d"], 1)
            gamma_out(0)
            group_scales(0, 0, reused=False)
            quantise_high(0, 0, reused=False)
            gamma_out(1)
            group_scales(1, 1, reused=False)
            quantise_high(1, 1, reused=False)
            for t in range(2, 4):
                gamma_out(t)
            v.wait_ge(S["ctx_mm"], 1)
            v.wait_ge(S["ctx_zero"], 1)

            def ctx_norm(k):
                own(v.reciprocal(krec[:, k:k + 1], bank[2 + k][:, 128:129]))
                if k >= 2:
                    v.wait_ge(S["ctxT_mm"], k - 1)
                v.tensor_scalar(ctxn[:, k % 2, :], bank[2 + k][:, 0:128], krec[:, k:k + 1], 1.0 / X_SCALE, ALU.mult, ALU.mult).then_inc(S["ctx_n"], 1)

            ctx_norm(0)
            for k in range(K):
                v.wait_ge(S["ctx_hi"], k + 1)
                for h in range(2):
                    d = slice(64 * h, 64 * h + 64)
                    ins = v.scalar_tensor_tensor(ctxT[d, k % 2, 1, d], bank[6][d, d], C_SCALE, ctxT[d, k % 2, 0, d], ALU.mult, ALU.subtract)
                ins.then_inc(S["ctx_lo"], 1)
                if k + 1 < K:
                    ctx_norm(k + 1)
                gamma_out(4 + k)
                v.wait_ge(S["w2_hi"], k + 1)
                v.scalar_tensor_tensor(w2[:, 1, k, :], bank[7][:, :], 1.0 / W_SCALE, w2[:, 0, k, :], ALU.mult, ALU.subtract).then_inc(S["w2_lo"], 1)
            gamma_out(8)

            def mix_stats(t):
                v.wait_ge(S["mix_mm"], t + 1)
                if t >= 2:
                    v.wait_ge(S["mst_p"], t - 1)
                own(v.bn_stats(st6[:, t, :], bank[2 + t % 2][0:P, :]))
                v.bn_aggr(mst[:, t % 2, 0:2], st6[:, t, :]).then_inc(S["mst_v"], 1)

            def x1_sum(t):
                v.wait_ge(S["mix_g"], t + 1)
                v.wait_ge(S["gam_d"], t + 1)
                v.tensor_tensor(xr[:, t, :], xr[:, t, :], xn[:, t % 2, :], ALU.add).then_inc(S["x1_d"], 1)
                v.wait_ge(S["x1_d"], t + 1)
                own(v.bn_stats(st6x[:, t, :], xr[:, t, :]))
                if t >= 2:
                    v.wait_ge(S["x2_n"], t - 1)
                v.bn_aggr(xst[:, t % 2, 0:2], st6x[:, t, :]).then_inc(S["x1_st"], 1)

            def x2_low(t):
                v.wait_ge(S["x2_hi"], t + 1)
                d = slice(t * P, (t + 1) * P)
                v.scalar_tensor_tensor(qT[:, 1, :, d], tiles(bank[4 + t % 2]), X_SCALE, qT[:, 0, :, d], ALU.mult, ALU.subtract).then_inc(S["x2_lo"], 1)

            def w_low(i, g, half, u):
                v.wait_ge(S["wr_hi"], u + (g + 1))
                d = slice(g * D, (g + 1) * D)
                hi, lo = [(wgu[:, half, a, d] if g < 2 else hidden(wdT, a, i)) for a in range(2)]
                v.scalar_tensor_tensor(lo, bank[6 + (3 * half + g) % 2][:, :], W_SCALE, hi, ALU.mult, ALU.subtract).then_inc(S["wr_lo"], 1)

            for t in range(NT + 2):
                if t < NT:
                    mix_stats(t)
                if t == 1:
                    gamma_out(9)
                if 2 <= t < NT + 2:
                    x1_sum(t - 2)
                if 5 <= t:
                    x2_low(t - 5)
                if t == NT + 1:
                    group_scales(2, 0)
                if 3 <= t < 9:
                    i = (t - 3) // 3
                    w_low(i, (t - 3) % 3, i, 3 * i)
            x2_low(NT - 3)

            def gated(i, half, u, turn=True, first=False):
                for c, (n0, nn) in enumerate(NC3):
                    if first and c == 1:
                        x2_low(NT - 2)
                        x2_low(NT - 1)
                        quantise_high(2, 0)
                    slot = (half + c) % 2
                    v.wait_ge(S["sg_d"], u + (c + 1))
                    if not first or c == 2:
                        v.wait_ge(S["h_hi"], u + (c - 1))
                    v.scalar_tensor_tensor(hf[:, slot, 0:nn], bank[2 * c + 1][:, 0:nn], H_SCALE * UNDO, sg[:, slot, 0:nn], ALU.mult, ALU.mult).then_inc(S["hf_d"], 1)
                    v.wait_ge(S["h_hi"], u + (c + 1))
                    hi, lo = [hidden(hT, a, i)[:, n0:n0 + nn] for a in range(2)]
                    v.tensor_tensor(lo, hf[:, slot, 0:nn], hi, ALU.subtract).then_inc(S["h_lo"], 1)
                    if turn:
                        w_low(i + 1, c, 1 - half, u + 3)

            gated(0, 0, 0, turn=False, first=True)
            with v.Fori(1, FT - 2, 2) as i:
                for e in range(2):
                    group_scales(i + (2 + e), 1 - e)
                    quantise_high(i + (2 + e), 1 - e)
                    gated(i + e, 1 - e, i * 3 + 3 * e)
            gated(FT - 2, 1, 3 * (FT - 2))
            gated(FT - 1, 0, 3 * (FT - 1), turn=False)
            for t in range(NT):
                v.wait_ge(S["dn_mm"], t + 1)
                v.scalar_tensor_tensor(xr[:, t, :], bank[t % 2][0:P, :], 1.0 / (W_SCALE * H_SCALE), xr[:, t, :], ALU.mult, ALU.add).then_inc(S["dn_d"], 1)



_INS = ["x", "src", "dst", "L0_gnn_wc", "L0_gnn_wn", "L0_gnn_bias", "L0_mix_norm_gamma", "L0_mix_w_qkv", "L0_mix_w_out",
        "L0_mix_out_gamma", "L0_ffn_w_gate", "L0_ffn_w_up", "L0_ffn_w_down"]


def kernel(**inputs):
    import numpy as np
    import concourse.bacc as bacc
    import concourse.bass_utils as bass_utils

    nc = bacc.Bacc("TRN2", target_bir_lowering=False, num_devices=1)
    arrays, args = {}, []
    for name in _INS:
        a = np.ascontiguousarray(inputs[name])
        arrays[f"in_{name}"] = a
        args.append(nc.dram_tensor(f"in_{name}", a.shape, mybir.dt.from_np(a.dtype), kind="ExternalInput").ap())
    out = nc.dram_tensor("out", inputs["x"].shape, F32, kind="ExternalOutput").ap()
    gps_layer(nc, *args, out)
    return bass_utils.run_bass_kernel_spmd(nc, [arrays], core_ids=[0]).results[0]["out"]
```
